# Optimizing a Trainium2 kernel written in Bass

```python
import numpy as np
import jax
import jax.numpy as jnp

def _softmax(x, axis=-1):
    return jax.nn.softmax(x, axis=axis)

def _gelu(x):
    return jax.nn.gelu(x, approximate=True)

def _silu(x):
    return jax.nn.silu(x)

def _sigmoid(x):
    return jax.nn.sigmoid(x)

def _layernorm(x, axis=-1, eps=1e-05):
    m = jnp.mean(x, axis=axis, keepdims=True)
    v = jnp.var(x, axis=axis, keepdims=True)
    return (x - m) / jnp.sqrt(v + eps)

def _scatter_add(tgt, idx, src, axis=0):
    return tgt.at[idx].add(src)

def _segment_sum(src, seg, n):
    return jax.ops.segment_sum(src, seg, n)
kernel_name = 'mk_perceiver_d2_seqx_r4_42bd12'

def setup_inputs(seed: int=0):
    np.random.seed(seed)
    _w = jnp.asarray

    def _rec_inputs():
        import jax
        import jax.numpy as jnp
        _rk = jax.random.key(seed)
        x = -0.0002928 + 1 * jax.random.normal(jax.random.fold_in(_rk, 1), (1, 128, 256), jnp.float32)
        _lenS = 128 - jax.random.randint(jax.random.fold_in(_rk, 7), (1,), 0, max(1, 128 // 4) + 1, jnp.int32)
        _lenS2 = 12544 - jax.random.randint(jax.random.fold_in(_rk, 8), (1,), 0, max(1, 12544 // 4) + 1, jnp.int32)
        _ctx_1024P = jax.random.normal(jax.random.fold_in(_rk, 11), (1, 16, 256), jnp.float32)
        _ctx_1024c = jax.random.dirichlet(jax.random.fold_in(_rk, 511), 0.3 * jnp.ones((16,), jnp.float32), (1, 12544))
        _ctx_1024t = jnp.einsum('bsk,bkd->bsd', _ctx_1024c, _ctx_1024P)
        _ctx_1024t = _ctx_1024t * jax.lax.rsqrt(jnp.mean(jnp.square(_ctx_1024t)) + 1e-12) * 0.953939
        ctx_1024 = 0.000227908 + 0.99994 * (_ctx_1024t + 0.3 * jax.random.normal(jax.random.fold_in(_rk, 611), (1, 12544, 256), jnp.float32))
        _validS = jnp.arange(128)[None, :] < _lenS[:, None]
        _validS2 = jnp.arange(12544)[None, :] < _lenS2[:, None]
        _causal = jnp.tril(jnp.ones((128, 128), dtype=bool))
        mask_SxS_bc0 = jnp.logical_not(jnp.broadcast_to(_causal[:, :], (128, 128)))
        return (x, ctx_1024, mask_SxS_bc0)
    x, ctx_1024, mask_SxS_bc0 = _rec_inputs()

    def _L0_xattn_setup():
        import jax, jax.numpy as jnp
        import numpy as np
        from jax import lax
        H = 16
        K1, K2 = (3, 3)
        LN_EPS = 1e-05

        def _ln(x, g, b):
            m = jnp.mean(x, axis=-1, keepdims=True)
            v = jnp.mean(jnp.square(x - m), axis=-1, keepdims=True)
            return (x - m) * lax.rsqrt(v + LN_EPS) * g + b

        def _gelu(x):
            return jax.nn.gelu(x, approximate=False)
        key = jax.random.key(seed)
        B, T, D, Th = (4, 256, 256, 64)
        C = 2 * D
        ks = jax.random.split(key, 16)

        def w(k, shape):
            fan_in = shape[0]
            return (jax.random.normal(k, shape, jnp.float32) / np.sqrt(fan_in)).astype(jnp.float32)
        inp = {'x': jax.random.normal(ks[0], (B, T, D), jnp.float32), 'historical_data': jax.random.normal(ks[1], (B, Th, D), jnp.float32), 'Wq': w(ks[2], (D, D)), 'Wk': w(ks[3], (D, D)), 'Wv': w(ks[4], (D, D)), 'hist_W': w(ks[5], (D, C)), 'hist_b': jnp.zeros((C,), jnp.float32), 'hist_ln_g': jnp.ones((C,), jnp.float32), 'hist_ln_b': jnp.zeros((C,), jnp.float32), 'ctx_W1': w(ks[6], (C, C // 4)), 'ctx_b1': jnp.zeros((C // 4,), jnp.float32), 'ctx_W2': w(ks[7], (C // 4, 1)), 'ctx_b2': jnp.zeros((1,), jnp.float32), 'kg_W1': w(ks[8], (C, D)), 'kg_b1': jnp.zeros((D,), jnp.float32), 'kg_ln_g': jnp.ones((D,), jnp.float32), 'kg_ln_b': jnp.zeros((D,), jnp.float32), 'kg_W2': w(ks[9], (D, H * K1 * K2)), 'kg_b2': jnp.zeros((H * K1 * K2,), jnp.float32), 'proj_W': w(ks[10], (D, D)), 'proj_b': jnp.zeros((D,), jnp.float32), 'causal_mask': jnp.triu(jnp.ones((T, T), bool), k=1)}
        return inp
    _L0_xattn_all = _L0_xattn_setup()
    _L0_xattn_in = {k: v for k, v in _L0_xattn_all.items() if k in ('Wq', 'Wk', 'Wv', 'hist_W', 'hist_b', 'hist_ln_g', 'hist_ln_b', 'ctx_W1', 'ctx_b1', 'ctx_W2', 'ctx_b2', 'kg_W1', 'kg_b1', 'kg_ln_g', 'kg_ln_b', 'kg_W2', 'kg_b2', 'proj_W', 'proj_b')}
    del _L0_xattn_all

    def _L0_attn_setup():
        import jax, jax.numpy as jnp
        import numpy as np
        B, N, HID = (8, 1024, 256)
        HEADS = 16
        D = HID // HEADS
        LN_EPS = 1e-05
        key = jax.random.key(seed)
        ks = jax.random.split(key, 8)
        s = 1.0 / np.sqrt(HID)
        x = jax.random.normal(ks[0], (B, N, HID), dtype=jnp.float32)
        Wh = jax.random.uniform(ks[1], (HID, HID), jnp.float32, -s, s)
        Wq = jax.random.uniform(ks[2], (HID, HID), jnp.float32, -s, s)
        Wk = jax.random.uniform(ks[3], (HID, HID), jnp.float32, -s, s)
        Wv = jax.random.uniform(ks[4], (HID, HID), jnp.float32, -s, s)
        Wo = jax.random.uniform(ks[5], (HID, HID), jnp.float32, -s, s)
        bh = jax.random.uniform(ks[6], (HID,), jnp.float32, -s, s)
        bq = jnp.zeros((HID,), jnp.float32)
        bk = jnp.zeros((HID,), jnp.float32)
        bv = jnp.zeros((HID,), jnp.float32)
        bo = jax.random.uniform(ks[7], (HID,), jnp.float32, -s, s)
        beta = jnp.full((HID,), 0.1, jnp.float32)
        ln_w = jnp.ones((HID,), jnp.float32)
        ln_b = jnp.zeros((HID,), jnp.float32)
        return {'x': x, 'Wh': Wh, 'bh': bh, 'Wq': Wq, 'bq': bq, 'Wk': Wk, 'bk': bk, 'Wv': Wv, 'bv': bv, 'beta': beta, 'ln_w': ln_w, 'ln_b': ln_b, 'Wo': Wo, 'bo': bo}
    _L0_attn_all = _L0_attn_setup()
    _L0_attn_in = {k: v for k, v in _L0_attn_all.items() if k in ('Wh', 'bh', 'Wq', 'bq', 'Wk', 'bk', 'Wv', 'bv', 'beta', 'ln_w', 'ln_b', 'Wo', 'bo')}
    del _L0_attn_all

    def _L0_ffn_setup():
        import jax, jax.numpy as jnp
        import numpy as np
        DIM = 256
        MOE_HID = 128
        SHARED_HID = 512
        N_EXPERTS = 16
        TOP_K = 2
        NORM_TOPK_PROB = True
        key = jax.random.key(seed)
        ks = jax.random.split(key, 9)
        s = 0.02
        x = jax.random.normal(ks[0], (2, 256, DIM), dtype=jnp.float32)
        Wg = jax.random.normal(ks[1], (N_EXPERTS, DIM), dtype=jnp.float32) * s
        We_gate = jax.random.normal(ks[2], (N_EXPERTS, MOE_HID, DIM), dtype=jnp.float32) * s
        We_up = jax.random.normal(ks[3], (N_EXPERTS, MOE_HID, DIM), dtype=jnp.float32) * s
        We_down = jax.random.normal(ks[4], (N_EXPERTS, DIM, MOE_HID), dtype=jnp.float32) * s
        Ws_gate = jax.random.normal(ks[5], (SHARED_HID, DIM), dtype=jnp.float32) * s
        Ws_up = jax.random.normal(ks[6], (SHARED_HID, DIM), dtype=jnp.float32) * s
        Ws_down = jax.random.normal(ks[7], (DIM, SHARED_HID), dtype=jnp.float32) * s
        Wsg = jax.random.normal(ks[8], (1, DIM), dtype=jnp.float32) * s
        return {'x': x, 'Wg': Wg, 'We_gate': We_gate, 'We_up': We_up, 'We_down': We_down, 'Ws_gate': Ws_gate, 'Ws_up': Ws_up, 'Ws_down': Ws_down, 'Wsg': Wsg}
    _L0_ffn_all = _L0_ffn_setup()
    _L0_ffn_in = {k: v for k, v in _L0_ffn_all.items() if k in ('Wg', 'We_gate', 'We_up', 'We_down', 'Ws_gate', 'Ws_up', 'Ws_down', 'Wsg')}
    del _L0_ffn_all

    def _L1_xattn_setup():
        import jax, jax.numpy as jnp
        import numpy as np
        B, L, S, D, H = (4, 512, 512, 256, 16)
        E = D // H
        key = jax.random.key(seed)
        ks = jax.random.split(key, 7)
        sc = 1.0 / np.sqrt(D)
        return {'q': jax.random.normal(ks[0], (B, L, D), dtype=jnp.float32), 'k': jax.random.normal(ks[1], (B, S, D), dtype=jnp.float32), 'v': jax.random.normal(ks[2], (B, S, D), dtype=jnp.float32), 'Wq': jax.random.normal(ks[3], (D, D), dtype=jnp.float32) * sc, 'bq': jnp.zeros((D,), dtype=jnp.float32), 'Wo': jax.random.normal(ks[4], (D, D), dtype=jnp.float32) * sc, 'bo': jnp.zeros((D,), dtype=jnp.float32)}
    _L1_xattn_all = _L1_xattn_setup()
    _L1_xattn_in = {k: v for k, v in _L1_xattn_all.items() if k in ('Wq', 'bq', 'Wo', 'bo')}
    del _L1_xattn_all

    def _L1_attn_setup():
        import jax, jax.numpy as jnp
        import numpy as np
        NHEADS = 16
        SCALE_BASE = 128
        GN_EPS = 1e-05

        def rotate_every_two(x):
            x1 = x[..., ::2]
            x2 = x[..., 1::2]
            return jnp.stack((-x2, x1), axis=-1).reshape(x.shape)

        def xpos_apply(x, downscale, offset=0):
            B, T, C = x.shape
            half = C // 2
            scale_vec = (jnp.arange(0, C, 2, dtype=jnp.float32) + 0.4 * C) / (1.4 * C)
            min_pos = -(T + offset) // 2
            max_pos = T + offset + min_pos
            power = jnp.arange(min_pos, max_pos, dtype=jnp.float32) / SCALE_BASE
            scale = scale_vec[None, :] ** power[:, None]
            L = scale.shape[0]
            inv_freq = 1.0 / 10000.0 ** (jnp.arange(half, dtype=jnp.float32) / half)
            sinusoid = jnp.arange(L, dtype=jnp.float32)[:, None] * inv_freq[None, :]
            sin, cos = (jnp.sin(sinusoid), jnp.cos(sinusoid))
            if L > T:
                scale, sin, cos = (scale[-T:], sin[-T:], cos[-T:])
            if downscale:
                scale = 1.0 / scale
            sin = jnp.repeat(sin * scale, 2, axis=-1)
            cos = jnp.repeat(cos * scale, 2, axis=-1)
            return x * cos + rotate_every_two(x) * sin

        def decay_mask(nheads, T):
            gamma = 1.0 - 2.0 ** (-5.0 - jnp.arange(nheads, dtype=jnp.float32))
            idx = jnp.arange(T)
            diff = idx[:, None] - idx[None, :]
            keep = diff >= 0
            m = gamma[:, None, None] ** jnp.where(keep, diff, 0).astype(jnp.float32)
            return jnp.where(keep[None, :, :], m, 0.0)
        key = jax.random.key(seed)
        ks = jax.random.split(key, 6)
        B, T, C = (2, 512, 256)
        w_std = 0.02
        return {'x': jax.random.normal(ks[0], (B, T, C), jnp.float32), 'w_qkvff': jax.random.normal(ks[1], (5 * C, C), jnp.float32) * w_std, 'w_gated': jax.random.normal(ks[2], (C, C), jnp.float32) * w_std, 'b_gated': jnp.zeros((C,), jnp.float32), 'w_proj': jax.random.normal(ks[3], (C, C), jnp.float32) * w_std, 'b_proj': jnp.zeros((C,), jnp.float32), 'gn_w': jnp.ones((C,), jnp.float32), 'gn_b': jnp.zeros((C,), jnp.float32), 'w_ff': jax.random.normal(ks[4], (C, 2 * C), jnp.float32) * w_std, 'rms_w': jnp.ones((C,), jnp.float32)}
    _L1_attn_all = _L1_attn_setup()
    _L1_attn_in = {k: v for k, v in _L1_attn_all.items() if k in ('w_qkvff', 'w_gated', 'b_gated', 'w_proj', 'b_proj', 'gn_w', 'gn_b', 'w_ff', 'rms_w')}
    del _L1_attn_all

    def _L1_ffn_setup():
        import jax, jax.numpy as jnp
        import numpy as np
        D_MODEL, D_FF, RANK = (256, 1024, 64)
        B, S = (4, 1024)
        key = jax.random.key(seed)
        ks = jax.random.split(key, 7)
        return {'x': jax.random.normal(ks[0], (B, S, D_MODEL), dtype=jnp.float32), 'U1': jax.random.normal(ks[1], (D_MODEL, RANK), dtype=jnp.float32) * 0.02, 'V1': jax.random.normal(ks[2], (RANK, D_FF), dtype=jnp.float32) * 0.02, 'b1': jnp.zeros((D_FF,), dtype=jnp.float32), 'U2': jax.random.normal(ks[3], (D_FF, RANK), dtype=jnp.float32) * 0.02, 'V2': jax.random.normal(ks[4], (RANK, D_MODEL), dtype=jnp.float32) * 0.02, 'b2': jnp.zeros((D_MODEL,), dtype=jnp.float32)}
    _L1_ffn_all = _L1_ffn_setup()
    _L1_ffn_in = {k: v for k, v in _L1_ffn_all.items() if k in ('U1', 'V1', 'b1', 'U2', 'V2', 'b2')}
    del _L1_ffn_all
    return {'x': x, 'ctx_1024': ctx_1024, 'mask_SxS_bc0': mask_SxS_bc0, 'L0_xattn_Wq': _L0_xattn_in['Wq'], 'L0_xattn_Wk': _L0_xattn_in['Wk'], 'L0_xattn_Wv': _L0_xattn_in['Wv'], 'L0_xattn_hist_W': _L0_xattn_in['hist_W'], 'L0_xattn_hist_b': _L0_xattn_in['hist_b'], 'L0_xattn_hist_ln_g': _L0_xattn_in['hist_ln_g'], 'L0_xattn_hist_ln_b': _L0_xattn_in['hist_ln_b'], 'L0_xattn_ctx_W1': _L0_xattn_in['ctx_W1'], 'L0_xattn_ctx_b1': _L0_xattn_in['ctx_b1'], 'L0_xattn_ctx_W2': _L0_xattn_in['ctx_W2'], 'L0_xattn_ctx_b2': _L0_xattn_in['ctx_b2'], 'L0_xattn_kg_W1': _L0_xattn_in['kg_W1'], 'L0_xattn_kg_b1': _L0_xattn_in['kg_b1'], 'L0_xattn_kg_ln_g': _L0_xattn_in['kg_ln_g'], 'L0_xattn_kg_ln_b': _L0_xattn_in['kg_ln_b'], 'L0_xattn_kg_W2': _L0_xattn_in['kg_W2'], 'L0_xattn_kg_b2': _L0_xattn_in['kg_b2'], 'L0_xattn_proj_W': _L0_xattn_in['proj_W'], 'L0_xattn_proj_b': _L0_xattn_in['proj_b'], 'L0_attn_Wh': _L0_attn_in['Wh'], 'L0_attn_bh': _L0_attn_in['bh'], 'L0_attn_Wq': _L0_attn_in['Wq'], 'L0_attn_bq': _L0_attn_in['bq'], 'L0_attn_Wk': _L0_attn_in['Wk'], 'L0_attn_bk': _L0_attn_in['bk'], 'L0_attn_Wv': _L0_attn_in['Wv'], 'L0_attn_bv': _L0_attn_in['bv'], 'L0_attn_beta': _L0_attn_in['beta'], 'L0_attn_ln_w': _L0_attn_in['ln_w'], 'L0_attn_ln_b': _L0_attn_in['ln_b'], 'L0_attn_Wo': _L0_attn_in['Wo'], 'L0_attn_bo': _L0_attn_in['bo'], 'L0_ffn_Wg': _L0_ffn_in['Wg'], 'L0_ffn_We_gate': _L0_ffn_in['We_gate'], 'L0_ffn_We_up': _L0_ffn_in['We_up'], 'L0_ffn_We_down': _L0_ffn_in['We_down'], 'L0_ffn_Ws_gate': _L0_ffn_in['Ws_gate'], 'L0_ffn_Ws_up': _L0_ffn_in['Ws_up'], 'L0_ffn_Ws_down': _L0_ffn_in['Ws_down'], 'L0_ffn_Wsg': _L0_ffn_in['Wsg'], 'L1_xattn_Wq': _L1_xattn_in['Wq'], 'L1_xattn_bq': _L1_xattn_in['bq'], 'L1_xattn_Wo': _L1_xattn_in['Wo'], 'L1_xattn_bo': _L1_xattn_in['bo'], 'L1_attn_w_qkvff': _L1_attn_in['w_qkvff'], 'L1_attn_w_gated': _L1_attn_in['w_gated'], 'L1_attn_b_gated': _L1_attn_in['b_gated'], 'L1_attn_w_proj': _L1_attn_in['w_proj'], 'L1_attn_b_proj': _L1_attn_in['b_proj'], 'L1_attn_gn_w': _L1_attn_in['gn_w'], 'L1_attn_gn_b': _L1_attn_in['gn_b'], 'L1_attn_w_ff': _L1_attn_in['w_ff'], 'L1_attn_rms_w': _L1_attn_in['rms_w'], 'L1_ffn_U1': _L1_ffn_in['U1'], 'L1_ffn_V1': _L1_ffn_in['V1'], 'L1_ffn_b1': _L1_ffn_in['b1'], 'L1_ffn_U2': _L1_ffn_in['U2'], 'L1_ffn_V2': _L1_ffn_in['V2'], 'L1_ffn_b2': _L1_ffn_in['b2']}

def reference(x, ctx_1024, mask_SxS_bc0, L0_xattn_Wq, L0_xattn_Wk, L0_xattn_Wv, L0_xattn_hist_W, L0_xattn_hist_b, L0_xattn_hist_ln_g, L0_xattn_hist_ln_b, L0_xattn_ctx_W1, L0_xattn_ctx_b1, L0_xattn_ctx_W2, L0_xattn_ctx_b2, L0_xattn_kg_W1, L0_xattn_kg_b1, L0_xattn_kg_ln_g, L0_xattn_kg_ln_b, L0_xattn_kg_W2, L0_xattn_kg_b2, L0_xattn_proj_W, L0_xattn_proj_b, L0_attn_Wh, L0_attn_bh, L0_attn_Wq, L0_attn_bq, L0_attn_Wk, L0_attn_bk, L0_attn_Wv, L0_attn_bv, L0_attn_beta, L0_attn_ln_w, L0_attn_ln_b, L0_attn_Wo, L0_attn_bo, L0_ffn_Wg, L0_ffn_We_gate, L0_ffn_We_up, L0_ffn_We_down, L0_ffn_Ws_gate, L0_ffn_Ws_up, L0_ffn_Ws_down, L0_ffn_Wsg, L1_xattn_Wq, L1_xattn_bq, L1_xattn_Wo, L1_xattn_bo, L1_attn_w_qkvff, L1_attn_w_gated, L1_attn_b_gated, L1_attn_w_proj, L1_attn_b_proj, L1_attn_gn_w, L1_attn_gn_b, L1_attn_w_ff, L1_attn_rms_w, L1_ffn_U1, L1_ffn_V1, L1_ffn_b1, L1_ffn_U2, L1_ffn_V2, L1_ffn_b2):
    import jax
    import jax.numpy as jnp

    def _L0_xattn_ref(x, historical_data, Wq, Wk, Wv, hist_W, hist_b, hist_ln_g, hist_ln_b, ctx_W1, ctx_b1, ctx_W2, ctx_b2, kg_W1, kg_b1, kg_ln_g, kg_ln_b, kg_W2, kg_b2, proj_W, proj_b, causal_mask):
        import jax, jax.numpy as jnp
        import numpy as np
        from jax import lax
        H = 16
        K1, K2 = (3, 3)
        LN_EPS = 1e-05

        def _ln(x, g, b):
            m = jnp.mean(x, axis=-1, keepdims=True)
            v = jnp.mean(jnp.square(x - m), axis=-1, keepdims=True)
            return (x - m) * lax.rsqrt(v + LN_EPS) * g + b

        def _gelu(x):
            return jax.nn.gelu(x, approximate=False)
        B, T, D = x.shape
        hd = D // H
        scale = hd ** (-0.5)
        q = (x @ Wq).reshape(B, T, H, hd).transpose(0, 2, 1, 3)
        k = (x @ Wk).reshape(B, T, H, hd).transpose(0, 2, 1, 3)
        v = (x @ Wv).reshape(B, T, H, hd).transpose(0, 2, 1, 3)
        attn = jnp.einsum('bhqd,bhkd->bhqk', q, k) * scale
        eh = _gelu(_ln(historical_data @ hist_W + hist_b, hist_ln_g, hist_ln_b))
        aw = _gelu(eh @ ctx_W1 + ctx_b1) @ ctx_W2 + ctx_b2
        aw = jax.nn.softmax(aw, axis=1)
        cc = jnp.sum(eh * aw, axis=1)
        kp = _gelu(_ln(cc @ kg_W1 + kg_b1, kg_ln_g, kg_ln_b)) @ kg_W2 + kg_b2
        kernels = jax.nn.softmax(kp.reshape(B, H, K1 * K2), axis=-1)
        kernels = kernels.reshape(B * H, 1, K1, K2)
        mask = causal_mask[None, None]
        attn0 = jnp.where(mask, 0.0, attn).reshape(1, B * H, T, T)
        attn = lax.conv_general_dilated(attn0, kernels, window_strides=(1, 1), padding=((K1 // 2, K1 // 2), (K2 // 2, K2 // 2)), feature_group_count=B * H, dimension_numbers=('NCHW', 'OIHW', 'NCHW')).reshape(B, H, T, T)
        attn = jnp.where(mask, -jnp.inf, attn)
        p = jax.nn.softmax(attn, axis=-1)
        out = jnp.einsum('bhqk,bhkd->bhqd', p, v)
        out = out.transpose(0, 2, 1, 3).reshape(B, T, D)
        return out @ proj_W + proj_b

    def _L0_attn_ref(x, Wh, bh, Wq, bq, Wk, bk, Wv, bv, beta, ln_w, ln_b, Wo, bo):
        import jax, jax.numpy as jnp
        import numpy as np
        B, N, HID = (8, 1024, 256)
        HEADS = 16
        D = HID // HEADS
        LN_EPS = 1e-05
        b, n, _ = x.shape
        h = x @ Wh + bh
        q = jax.nn.sigmoid(x @ Wq + bq).reshape(b, n, D, HEADS)
        k = jax.nn.sigmoid(x @ Wk + bk).reshape(b, n, D, HEADS)
        v = (x @ Wv + bv).reshape(b, n, D, HEADS)
        kv = jnp.einsum('bndh,bnmh->bdmh', k, v)
        num = jnp.einsum('bndh,bdmh->bnmh', q, kv)
        k_sum = jnp.einsum('bndh->bdh', k)
        den = jnp.einsum('bndh,bdh->bnh', q, k_sum)[:, :, None, :]
        attn = (num / den).reshape(b, n, HEADS * D)
        mu = jnp.mean(attn, axis=-1, keepdims=True)
        var = jnp.var(attn, axis=-1, keepdims=True)
        ln = (attn - mu) * jax.lax.rsqrt(var + LN_EPS) * ln_w + ln_b
        gated = ln * (h + beta)
        out = jax.nn.relu(gated @ Wo + bo)
        return out

    def _L0_ffn_ref(x, Wg, We_gate, We_up, We_down, Ws_gate, Ws_up, Ws_down, Wsg):
        import jax, jax.numpy as jnp
        import numpy as np
        DIM = 256
        MOE_HID = 128
        SHARED_HID = 512
        N_EXPERTS = 16
        TOP_K = 2
        NORM_TOPK_PROB = True
        B, S, D = x.shape
        xt = x.reshape(-1, D)
        gates = jax.nn.softmax(xt @ Wg.T, axis=-1)
        scores, inds = jax.lax.top_k(gates, TOP_K)
        if NORM_TOPK_PROB:
            scores = scores / jnp.sum(scores, axis=-1, keepdims=True)
        g = jnp.einsum('td,ehd->teh', xt, We_gate)
        u = jnp.einsum('td,ehd->teh', xt, We_up)
        h = jax.nn.silu(g) * u
        y_all = jnp.einsum('teh,edh->ted', h, We_down)
        y_sel = jnp.take_along_axis(y_all, inds[:, :, None], axis=1)
        y = jnp.sum(y_sel * scores[:, :, None], axis=1)
        shared = jax.nn.silu(xt @ Ws_gate.T) * (xt @ Ws_up.T) @ Ws_down.T
        y = y + jax.nn.sigmoid(xt @ Wsg.T) * shared
        return y.reshape(B, S, D)

    def _L1_xattn_ref(q, k, v, Wq, bq, Wo, bo):
        import jax, jax.numpy as jnp
        import numpy as np
        B, L, S, D, H = (4, 512, 512, 256, 16)
        E = D // H
        b, l, _ = q.shape
        s = k.shape[1]
        qp = (q @ Wq.T + bq).reshape(b, l, H, E)
        kp = (k @ Wq.T + bq).reshape(b, s, H, E)
        vp = (v @ Wq.T + bq).reshape(b, s, H, E)
        scale = 1.0 / np.sqrt(E)
        scores = jnp.einsum('blhe,bshe->bhls', qp, kp)
        attn = jax.nn.softmax(scale * scores, axis=-1)
        out = jnp.einsum('bhls,bshd->blhd', attn, vp)
        out = jnp.transpose(out, (0, 2, 1, 3)).reshape(b, l, H * E)
        return out @ Wo.T + bo

    def _L1_attn_ref(x, w_qkvff, w_gated, b_gated, w_proj, b_proj, gn_w, gn_b, w_ff, rms_w):
        import jax, jax.numpy as jnp
        import numpy as np
        NHEADS = 16
        SCALE_BASE = 128
        GN_EPS = 1e-05

        def rotate_every_two(x):
            x1 = x[..., ::2]
            x2 = x[..., 1::2]
            return jnp.stack((-x2, x1), axis=-1).reshape(x.shape)

        def xpos_apply(x, downscale, offset=0):
            B, T, C = x.shape
            half = C // 2
            scale_vec = (jnp.arange(0, C, 2, dtype=jnp.float32) + 0.4 * C) / (1.4 * C)
            min_pos = -(T + offset) // 2
            max_pos = T + offset + min_pos
            power = jnp.arange(min_pos, max_pos, dtype=jnp.float32) / SCALE_BASE
            scale = scale_vec[None, :] ** power[:, None]
            L = scale.shape[0]
            inv_freq = 1.0 / 10000.0 ** (jnp.arange(half, dtype=jnp.float32) / half)
            sinusoid = jnp.arange(L, dtype=jnp.float32)[:, None] * inv_freq[None, :]
            sin, cos = (jnp.sin(sinusoid), jnp.cos(sinusoid))
            if L > T:
                scale, sin, cos = (scale[-T:], sin[-T:], cos[-T:])
            if downscale:
                scale = 1.0 / scale
            sin = jnp.repeat(sin * scale, 2, axis=-1)
            cos = jnp.repeat(cos * scale, 2, axis=-1)
            return x * cos + rotate_every_two(x) * sin

        def decay_mask(nheads, T):
            gamma = 1.0 - 2.0 ** (-5.0 - jnp.arange(nheads, dtype=jnp.float32))
            idx = jnp.arange(T)
            diff = idx[:, None] - idx[None, :]
            keep = diff >= 0
            m = gamma[:, None, None] ** jnp.where(keep, diff, 0).astype(jnp.float32)
            return jnp.where(keep[None, :, :], m, 0.0)
        B, T, C = x.shape
        H = NHEADS
        hd = C // H
        nrm = jnp.sqrt(jnp.sum(x * x, axis=-1, keepdims=True)) * C ** (-0.5)
        x_ = x / jnp.maximum(nrm, 1e-08) * rms_w
        qkvff = jnp.einsum('btc,oc->bto', x_, w_qkvff)
        q, k, v, ff = jnp.split(qkvff, [C, 2 * C, 3 * C], axis=-1)
        q = xpos_apply(q, downscale=False)
        k = xpos_apply(k, downscale=True)
        q = q.reshape(B, T, H, hd).transpose(0, 2, 1, 3)
        k = k.reshape(B, T, H, hd).transpose(0, 2, 1, 3)
        v = v.reshape(B, T, H, hd).transpose(0, 2, 1, 3)
        scores = jnp.einsum('bhtd,bhsd->bhts', q, k) * hd ** (-0.5)
        scores = scores * decay_mask(H, T)[None]
        y = jnp.einsum('bhts,bhsd->bhtd', scores, v)
        yg = y.transpose(0, 2, 1, 3).reshape(B * T, H, hd)
        mu = jnp.mean(yg, axis=-1, keepdims=True)
        var = jnp.mean((yg - mu) ** 2, axis=-1, keepdims=True)
        yg = (yg - mu) / jnp.sqrt(var + GN_EPS)
        y = yg.reshape(B * T, C) * gn_w + gn_b
        y = y.reshape(B, T, C)
        y = jax.nn.silu(jnp.einsum('btc,oc->bto', x, w_gated) + b_gated) * y
        y = jnp.einsum('btc,oc->bto', y, w_proj) + b_proj
        ff_out = jnp.einsum('bte,ce->btc', jax.nn.gelu(ff, approximate=False), w_ff)
        return x + ff_out + y

    def _L1_ffn_ref(x, U1, V1, b1, U2, V2, b2):
        import jax, jax.numpy as jnp
        import numpy as np
        D_MODEL, D_FF, RANK = (256, 1024, 64)
        B, S = (4, 1024)
        P = jnp.einsum('bsd,dr->bsr', x, U1)
        H = jax.nn.gelu(jnp.einsum('bsr,rf->bsf', P, V1) + b1)
        Q = jnp.einsum('bsf,fr->bsr', H, U2)
        return jnp.einsum('bsr,rd->bsd', Q, V2) + b2
    x = x + _L0_xattn_ref(_layernorm(x, axis=-1), ctx_1024, L0_xattn_Wq, L0_xattn_Wk, L0_xattn_Wv, L0_xattn_hist_W, L0_xattn_hist_b, L0_xattn_hist_ln_g, L0_xattn_hist_ln_b, L0_xattn_ctx_W1, L0_xattn_ctx_b1, L0_xattn_ctx_W2, L0_xattn_ctx_b2, L0_xattn_kg_W1, L0_xattn_kg_b1, L0_xattn_kg_ln_g, L0_xattn_kg_ln_b, L0_xattn_kg_W2, L0_xattn_kg_b2, L0_xattn_proj_W, L0_xattn_proj_b, mask_SxS_bc0)
    x = x + _L0_attn_ref(_layernorm(x, axis=-1), L0_attn_Wh, L0_attn_bh, L0_attn_Wq, L0_attn_bq, L0_attn_Wk, L0_attn_bk, L0_attn_Wv, L0_attn_bv, L0_attn_beta, L0_attn_ln_w, L0_attn_ln_b, L0_attn_Wo, L0_attn_bo)
    x = x + _L0_ffn_ref(_layernorm(x, axis=-1), L0_ffn_Wg, L0_ffn_We_gate, L0_ffn_We_up, L0_ffn_We_down, L0_ffn_Ws_gate, L0_ffn_Ws_up, L0_ffn_Ws_down, L0_ffn_Wsg)
    x = x + _L1_xattn_ref(_layernorm(x, axis=-1), ctx_1024, ctx_1024, L1_xattn_Wq, L1_xattn_bq, L1_xattn_Wo, L1_xattn_bo)
    x = x + _L1_attn_ref(_layernorm(x, axis=-1), L1_attn_w_qkvff, L1_attn_w_gated, L1_attn_b_gated, L1_attn_w_proj, L1_attn_b_proj, L1_attn_gn_w, L1_attn_gn_b, L1_attn_w_ff, L1_attn_rms_w)
    x = x + _L1_ffn_ref(_layernorm(x, axis=-1), L1_ffn_U1, L1_ffn_V1, L1_ffn_b1, L1_ffn_U2, L1_ffn_V2, L1_ffn_b2)
    return x

_drawn_inputs = setup_inputs


def setup_inputs(seed=0):
    import zlib

    import numpy as np

    out = dict(_drawn_inputs(seed))
    spreads = {'L0_xattn_hist_b': (0.0, 0.8),
     'L0_xattn_hist_ln_g': (1.0, 0.6),
     'L0_xattn_hist_ln_b': (0.0, 0.8),
     'L0_xattn_ctx_b1': (0.0, 2.0),
     'L0_xattn_kg_b1': (0.0, 0.8),
     'L0_xattn_kg_ln_g': (1.0, 0.6),
     'L0_xattn_kg_ln_b': (0.0, 0.8),
     'L0_xattn_kg_b2': (0.0, 0.8),
     'L0_xattn_proj_b': (0.0, 0.1),
     'L0_attn_bq': (0.0, 2.0),
     'L0_attn_bk': (0.0, 2.0),
     'L0_attn_bv': (0.0, 0.1),
     'L0_attn_beta': (0.10000000149011612, 0.6),
     'L0_attn_ln_w': (1.0, 0.2),
     'L0_attn_ln_b': (0.0, 0.376),
     'L1_xattn_bq': (0.0, 0.393),
     'L1_xattn_bo': (0.0, 0.453),
     'L1_attn_b_gated': (0.0, 2.0),
     'L1_attn_b_proj': (0.0, 0.622),
     'L1_attn_gn_w': (1.0, 0.6),
     'L1_attn_gn_b': (0.0, 2.0),
     'L1_attn_rms_w': (1.0, 0.6),
     'L1_ffn_b1': (0.0, 0.8),
     'L1_ffn_b2': (0.0, 0.8)}
    factors = {'L0_xattn_ctx_W1': 8.0,
     'L0_xattn_ctx_W2': 8.0,
     'L0_attn_bh': 3.945,
     'L0_attn_Wq': 8.0,
     'L0_attn_Wk': 8.0,
     'L0_ffn_Wg': 8.0,
     'L0_ffn_We_gate': 7.34,
     'L0_ffn_We_up': 7.233,
     'L0_ffn_We_down': 7.239,
     'L0_ffn_Ws_gate': 5.38,
     'L0_ffn_Ws_up': 5.287,
     'L0_ffn_Ws_down': 5.371,
     'L0_ffn_Wsg': 8.0,
     'L1_ffn_U1': 8.0,
     'L1_ffn_V1': 8.0,
     'L1_ffn_U2': 8.0,
     'L1_ffn_V2': 8.0,
     'L1_attn_w_gated': 4.889,
     'L1_attn_w_ff': 3.053}
    for name, (base, spread) in spreads.items():
        noise = np.random.default_rng([zlib.crc32(name.encode()), seed]).standard_normal(out[name].shape)
        drawn = base * np.exp(spread * noise) if base else spread * noise
        out[name] = jnp.asarray(drawn.astype(out[name].dtype))
    for name, factor in factors.items():
        out[name] = (out[name] * factor).astype(out[name].dtype)
    return out
```

```python
from contextlib import ExitStack

import numpy as np
import concourse.bass as bass
from concourse import mybir

F32 = mybir.dt.float32
F32R = mybir.dt.float32r
U8 = mybir.dt.uint8
U32 = mybir.dt.uint32
ALU = mybir.AluOpType
ACT = mybir.ActivationFunctionType
AX_X = mybir.AxisListType.X

P = 128
T = 128
D = 256
KD = D // P
H = 16
HD = D // H
S = 12544
LN_EPS = 1e-5
NEG = -1.0e30
MIN_START = -3.0e38

CH = 224
NCH = S // CH
GC = 4
NGR = NCH // GC
GW = GC * CH
HB = CH // 2
C2 = 512
CT = C2 // P

DVE_HEADS = 12
ROW_TOKENS = D // HD

SC = 896
NJ = S // SC
KT = SC // P
SW = SC // 2
NG = H // 2
VW = HD + 1
UNITS = NG * KT
PAIRS = UNITS // 2
NPB = 4
PV_LAG = 2

ONE_ROW = 3 * 2 * HD
STACK = ONE_ROW + 1

CLEAR = 3584
MAX_BANKS, EXP_BANKS = (0, 1, 6), (4, 5)

E = 16
ER = 4
FH = 1024


class Steps:

    def __init__(self, sem, names):
        self.sem, self.names, self.at = sem, names.split(), 0

    def done(self, ins, name):
        assert self.names[self.at] == name, (self.names[self.at], name)
        self.at += 1
        ins.then_inc(self.sem, 1)

    def wait(self, eng, name):
        eng.wait_ge(self.sem, self.names.index(name) + 1)


def wait_at(eng, sem, value):
    if isinstance(value, int) and value <= 0:
        return
    eng.wait_ge(sem, value)


def bank_of(banks, n):
    return banks[n % len(banks)]


def bank_free(banks, count, n):
    before = n - 1
    while bank_of(banks, before % count) != bank_of(banks, n):
        before -= 1
    return before + 1


KEY_AT = (1, 5, 7, 9)
SUM1_AT = 3
VAL_AT = (11, 12, 13, 14, 15, 16, 17)
SUM0_AT = 18
MAX_AT = 20
PART_AT = 12
EARLY = 8
LATE_UNITS = [[v for v in range(EARLY, 2 * H) if (v - EARLY) * 17 // (2 * H - EARLY) == p] for p in range(PAIRS)]
EARLY_UNITS = [[v for v in range(EARLY) if MAX_AT + 1 + v * 7 // EARLY == p] for p in range(PAIRS)]
GROUP_END = [(KT * g + KT - 1) // 2 for g in range(NG)]
SCORE_BANKS = (0, 3, 5, 7)


def pack_columns(parts):
    at, out = 0, {}
    for name, width in parts:
        out[name] = (at, width)
        at += width
    return out, at

PE_STEPS = """
bias_mean xn1_t qkv0 scores0_0 scores0_1 scores0_2 scores0_3 shift_down0 shift_down1 shift_down2 shift_down3
shift_up0 shift_up1 shift_up2 shift_up3 kg1 kg_t kg2 prob_t0 prob_t1 prob_t2 prob_t3 pv0 o0_t proj0 xn2_t qkvh1
kv1 num_den gated1_t proj1 xn3_t gates expand0 expand1 contract0 expand2 contract1 expand3 contract2 expand4
contract3 contract4 xn4_t q4 q4_stack o1_t proj4 xn5_t xr_t gated5 qkv5 ff5 rot_t scores5_0 scores5_1 scores5_2
scores5_3 y5 y5_t proj5 xn6_t p6 h6 q6 out6"""
ACT_STEPS = """
kv0 down0_0 down0_1 down0_2 down0_3 up0_0 up0_1 up0_2 up0_3 g_w kg_h kern_e prob0_0 prob0_1 prob0_2 prob0_3 kq1
e_gate s_gate_e silu0 silu1 silu2 silu3 silu4 ffT gate1 hT"""
POOL_STEPS = """
half_power rstd1 rstd_kg conv rstd2 rstd_att rstd3 rstd4 c_zero rstd5 rms5 gn_rstd rstd6"""
DVE_STEPS = """
hist_constants hist_weights history_done var1 xn1 xT1 q_blocks0 att0_0 att0_1 att0_2 att0_3 g_shift cc_wide
var_kg kg_n kg_hT kern_shift kernels s_max s_max_rest probT0 probT1 probT2 probT3 o0 o0T x1 var2 xn2 xT2 v1
kv_blocks var_att gated1 gT x2 var3 xn3 xT3 g_neg hid0 hid1 mixed0 hid2 mixed1 hid3 mixed2 hid4 mixed3 x3 var4
xn4 xT4 stack_ready q4_parts q_base o1 o1T x5 var5 xn5 xT5 ss5 xr xrT rot k_blocks5 scoreT0 scoreT1 scoreT2
scoreT3 gn_var y5n yT x5b var6 xn6 xT6 pT qT2 x6"""


def head_columns():
    return np.array([(4 * q + 2 * m + hh) * HD + d
                     for m in range(KD) for q in range(4) for hh in range(2) for d in range(HD)])


CONST_COLS, N_CONST = pack_columns([
    ("ident", P), ("same_head", P), ("shift_down", P), ("shift_up", P), ("sel_high", 4 * P), ("sel_low", 4 * P),
    ("iota", E), ("pair_rows", 2)])
HIST_COLS, N_HIST = pack_columns([
    ("W", KD * C2), ("W1", CT * P), ("W2", 1), ("b", CT), ("g", CT), ("beta", CT), ("b1", 1), ("b2", 1)])
L0_COLS, N_L0 = pack_columns([
    ("x_q", KD * D), ("x_k", KD * D), ("x_v", KD * D), ("x_proj", KD * D), ("kg1", CT * D), ("kg2", KD * H * 9),
    ("a_kvh", KD * 3 * D), ("a_q", KD * D), ("a_o", KD * D), ("gates", KD * (E + 1)), ("a_bq", KD),
    ("kg_g", D), ("kg_b", D), ("beta", D), ("ln_w", D), ("ln_b", D)])
L0_ROWS, N_ROWS0 = pack_columns([("kg_b1", D), ("kg_b2", H * 9), ("proj_b", D), ("a_kvh", 3 * D), ("a_bo", D)])
FFN_COLS, N_FFN = pack_columns([
    ("gate", KD * E * P), ("up", KD * E * P), ("down", E * D), ("s_gate", KD * 4 * P), ("s_up", KD * 4 * P),
    ("s_down", 4 * D)])
L0_PIECES = NCH - 8
L0_PIECE = -(-(N_L0 + N_FFN) // L0_PIECES)
XW_COLS, N_XW = pack_columns([("x_w", KD * D), ("x_b", KD)])
L1_COLS, N_L1 = pack_columns([
    ("qkv", KD * 3 * D), ("ff", KD * 2 * D), ("gated", KD * D), ("proj", KD * D), ("w_ff", CT * D),
    ("rms", D), ("gn_w", D), ("gn_b", D), ("u1", KD * 64), ("b1", FH // P), ("u2", FH // P * 64)])
L1_ROWS, N_ROWS1 = pack_columns([("b_gated", D), ("b_proj", D), ("b2", D)])
V_COLS, N_V = pack_columns([("v1", FH), ("v2", D)])
TABLE_COLS, N_TABLES = pack_columns([("cos", 2 * D), ("sin", 2 * D), ("decay", H * T)])


def constants():
    out = np.zeros((P, N_CONST), np.float32)

    def put(name, values):
        at, width = CONST_COLS[name]
        out[:, at:at + width] = values

    r = np.arange(P)
    put("ident", np.eye(P))
    put("same_head", r[:, None] // HD == r[None, :] // HD)
    put("shift_down", r[:, None] + 1 == r[None, :])
    put("shift_up", r[:, None] - 1 == r[None, :])
    high, low = np.zeros((2, P, 4, P), np.float32)
    for q in range(4):
        for hh in range(2):
            for d in range(HD):
                src = 32 * q + HD * hh + d
                high[src, q, HD * hh + d] = high[src, q, 32 + HD * hh + d] = 1
                low[src, q, 64 + HD * hh + d] = 1
    put("sel_high", high.reshape(P, -1))
    put("sel_low", low.reshape(P, -1))
    put("iota", np.arange(E)[None])
    put("pair_rows", (r[:, None] < ONE_ROW) & (r[:, None] // HD % 2 == np.arange(2)))
    return out


def tables():
    f = np.float32
    half = D // 2
    scale_vec = (np.arange(0, D, 2, dtype=f) + f(0.4 * D)) / f(1.4 * D)
    power = np.arange(-T // 2, T - T // 2, dtype=f) / f(128)
    scale = (scale_vec[None, :] ** power[:, None]).astype(f)
    inv_freq = (f(1) / f(10000) ** (np.arange(half, dtype=f) / f(half))).astype(f)
    angle = (np.arange(T, dtype=f)[:, None] * inv_freq[None, :]).astype(f)
    out = np.zeros((T, N_TABLES), f)
    sign = np.tile(np.array([-1, 1], f), half)
    for n, sc in enumerate((scale, f(1) / scale)):
        out[:, n * D:(n + 1) * D] = np.repeat(np.cos(angle) * sc, 2, -1)
        out[:, (2 + n) * D:(3 + n) * D] = np.repeat(np.sin(angle) * sc, 2, -1) * sign
    gamma = 1.0 - 2.0 ** (-5.0 - np.arange(H, dtype=f))
    ahead = np.arange(T)[None, :] - np.arange(T)[:, None]
    m = np.where(ahead >= 0, gamma[:, None, None] ** np.maximum(ahead, 0).astype(f)[None], 0) * HD ** -0.5
    out[:, TABLE_COLS["decay"][0]:] = m.transpose(1, 0, 2).reshape(T, H * T)
    return out


def build_kernel(nc, ctx_t, x_in, mask_in, const_in, hist_in, l0_in, rows0_in, xw_in, x_bo_in, x_o_in, l1_in,
                 rows1_in, v_in, tables_in, out):
    with ExitStack() as outer:
        def sem(name):
            return outer.enter_context(nc.semaphore(name))

        def sb(name, shape, dt=F32, scope=outer):
            return scope.enter_context(nc.sbuf_tensor(name, shape, dt))

        bank = outer.enter_context(nc.psum_tensor("bank", [P, 8, 512], F32))
        const = sb("const", [P, N_CONST])
        x = sb("x", [P, D])
        xn = sb("xn", [P, D])
        xT = sb("xT", [P, KD, T])
        ones_row = sb("ones_row", [1, T])
        ones = sb("ones", [P, 1])
        half_power = sb("half_power", [P, 2])
        stats6 = sb("stats6", [P, 6])
        mv = sb("mv", [P, 2])
        var_eps = sb("var_eps", [P, 1])
        rstd = sb("rstd", [P, 1])
        gate_cell = sb("gate_cell", [1, 1])

        def part(tile, cols, name, k=None):
            at, width = cols[name]
            view = tile[:, at:at + width]
            return view if k is None else view.rearrange("p (k n) -> p k n", k=k)

        ident = part(const, CONST_COLS, "ident")
        same_head = part(const, CONST_COLS, "same_head")
        head_col = same_head.rearrange("p (h d) -> p h d", d=HD)[:, :, 0]
        iota = part(const, CONST_COLS, "iota")

        ab = ExitStack()
        w_l0 = sb("w_l0", [P, L0_PIECES * L0_PIECE], scope=ab)
        w0, wf = w_l0[:, 0:N_L0], w_l0[:, N_L0:N_L0 + N_FFN]
        rows0 = sb("rows0", [1, N_ROWS0], scope=ab)
        group_stats = sb("group_stats", [P, NGR, 6], scope=ab)
        la = ExitStack()
        hw = sb("hw", [P, N_HIST], scope=la)
        w_centered = sb("w_centered", [P, KD, C2], scope=la)
        w_high = sb("w_high", [P, KD, C2], F32R, scope=la)
        w_low = sb("w_low", [P, KD, C2], F32R, scope=la)
        w_mean = sb("w_mean", [P, KD], scope=la)
        b_mean = sb("b_mean", [P, 1], scope=la)
        b_centered = sb("b_centered", [P, CT], scope=la)
        inv_width = sb("inv_width", [P, P], scope=la)
        all_ones = sb("all_ones", [P, P], scope=la)
        w2_wide = sb("w2_wide", [P, P], scope=la)
        hc_raw = sb("hc_raw", [P, 2, KD, CH], scope=la)
        hc_high = sb("hc_high", [P, 2, KD, CH], F32R, scope=la)
        hc_low = sb("hc_low", [P, 2, KD, CH], F32R, scope=la)
        square = sb("square", [P, CT, CH], scope=la)
        square2 = sb("square2", [P, 2, CH], scope=la)
        square1 = sb("square1", [P, CH], scope=la)
        h_var = sb("h_var", [HB, 2], scope=la)
        h_rstd = sb("h_rstd", [HB, 2], scope=la)
        h_diag = sb("h_diag", [HB, 2, HB], scope=la)
        rstd_wide = sb("rstd_wide", [P, CH], scope=la)
        normed = sb("normed", [P, 2, CT, CH], scope=la)
        eh = sb("eh", [P, 2, CT, GW], scope=la)
        hidden = sb("hidden", [P, CH], scope=la)
        logits = sb("logits", [P, 2, GW], scope=la)
        weight = sb("weight", [P, 2, GW], scope=la)
        stat = sb("stat", [P, 2, 6], scope=la)
        la.close()
        lb = ExitStack()
        mask_bytes = sb("mask_bytes", [P, T // 4], U32, scope=lb)
        masked = sb("masked", [P, T], scope=lb)
        keep = sb("keep", [P, T], scope=lb)
        hide = sb("hide", [P, T], scope=lb)
        q_blocks = sb("q_blocks", [P, KD, 8, T], scope=lb)
        kT = sb("kT", [P, KD, T], scope=lb)
        v0 = sb("v0", [P, D], scope=lb)
        att = sb("att", [P, 3, H, T + 2], scope=lb)
        conv = sb("conv", [P, H, T], scope=lb)
        tap_part = sb("tap_part", [P, H - DVE_HEADS, T], scope=lb)
        probT = sb("probT", [P, H, T], scope=lb)
        g_max = sb("g_max", [P, 1], scope=lb)
        g_w = sb("g_w", [P, NGR], scope=lb)
        g_sum = sb("g_sum", [P, NGR], scope=lb)
        g_cc = sb("g_cc", [P, NGR, CT], scope=lb)
        g_one = sb("g_one", [P, 1], scope=lb)
        cc = sb("cc", [P, CT], scope=lb)
        cc_wide = sb("cc_wide", [P, CT, P], scope=lb)
        kg_n = sb("kg_n", [P, D], scope=lb)
        kg_h = sb("kg_h", [P, D], scope=lb)
        kg_hT = sb("kg_hT", [P, KD, P], scope=lb)
        kern = sb("kern", [P, H, 9], scope=lb)
        kern_m = sb("kern_m", [P, H], scope=lb)
        s_max = sb("s_max", [P, H], scope=lb)
        s_sum = sb("s_sum", [P, H], scope=lb)
        o0 = sb("o0", [P, D], scope=lb)
        oT = sb("oT", [P, KD, T], scope=lb)
        lb.close()
        lc = ExitStack()
        k_sig = sb("k_sig", [P, D], scope=lc)
        v_lin = sb("v_lin", [P, D], scope=lc)
        h_beta = sb("h_beta", [P, D], scope=lc)
        q_sig = sb("q_sig", [P, KD, T], scope=lc)
        kv = sb("kv", [P, KD, P], scope=lc)
        k_sum = sb("k_sum", [P, KD, P], scope=lc)
        den = sb("den", [P, D], scope=lc)
        att1 = sb("att1", [P, D], scope=lc)
        gT = sb("gT", [P, KD, T], scope=lc)
        lc.close()
        ld = ExitStack()
        e_gate = sb("e_gate", [P, E], scope=ld)
        e_log = sb("e_log", [P, E + 1], scope=ld)
        top8 = sb("top8", [P, 8], scope=ld)
        top_at = sb("top_at", [P, 8], U32, scope=ld)
        top_f = sb("top_f", [P, 8], scope=ld)
        chosen = sb("chosen", [P, E], scope=ld)
        g_neg = sb("g_neg", [P, 1], scope=ld)
        g_den = sb("g_den", [P, 1], scope=ld)
        score = sb("score", [P, E], scope=ld)
        s_gate = sb("s_gate", [P, 1], scope=ld)
        silu = sb("silu", [P, 2, ER, T], scope=ld)
        hid = sb("hid", [P, 2, ER, T], scope=ld)
        ld.close()
        ab.close()

        le = ExitStack()
        k_stack1 = sb("k_stack1", [P, NG, SC], F32R, scope=le)
        q_f = sb("q_f", [P, KD, T], scope=le)
        q_h = sb("q_h", [P, KD, T], F32R, scope=le)
        q_l = sb("q_l", [P, KD, T], scope=le)
        q_base = sb("q_base", [P, NG, 2 * T], F32R, scope=le)
        q_stack = sb("q_stack", [P, 2, NG, 2 * T], F32R, scope=le)
        vals = sb("vals", [P, 2, KT * H * VW + 16], scope=le)
        prob = sb("prob", [P, NPB, 2, 2 * T], scope=le)
        o_part = sb("o_part", [P, NG, T], scope=le)
        unit_max = sb("unit_max", [P, H, 2], scope=le)
        head_max = sb("head_max", [P, H], scope=le)
        neg_max = sb("neg_max", [P, 2, H], F32R, scope=le)
        neg_maxT = sb("neg_maxT", [H, T], F32R, scope=le)
        alpha_log = sb("alpha_log", [P, H], scope=le)
        alpha = sb("alpha", [P, H], scope=le)
        acc = sb("acc", [P, NG, 2, VW], scope=le)
        o_den = sb("o_den", [P, H], scope=le)
        o1 = sb("o1", [P, D], scope=le)
        o1T = sb("o1T", [HD, H * T], scope=le)
        sb("clear_of_layer_0", [P, CLEAR], scope=le)
        lg = ExitStack()
        x_wts = sb("x_wts", [P, N_XW], scope=lg)
        x_bo = sb("x_bo", [1, D], scope=lg)
        x_high = sb("x_high", [P, KD, D], F32R, scope=lg)
        x_low = sb("x_low", [P, KD, D], F32R, scope=lg)
        ident_r = sb("ident_r", [P, P], F32R, scope=lg)
        s_raw = sb("s_raw", [P, KD, SC], scope=lg)
        s_high = sb("s_high", [P, KD, SC], F32R, scope=lg)
        s_low = sb("s_low", [P, KD, SC], F32R, scope=lg)
        k_high = sb("k_high", [P, 2, KD, SC], F32R, scope=lg)
        k_low = sb("k_low", [P, 2, KD, SC], F32R, scope=lg)
        k_stack0 = sb("k_stack0", [P, NG, SC], F32R, scope=lg)
        k_stack = (k_stack0, k_stack1)
        lg.close()
        lh = ExitStack()
        sb("after_x_bo", [P, N_XW + D], scope=lh)
        w1 = sb("w1", [P, N_L1], scope=lh)
        v_w = sb("v_w", [64, N_V], scope=lh)
        rows1 = sb("rows1", [1, N_ROWS1], scope=lh)
        x_o = sb("x_o", [HD, ROW_TOKENS, D], scope=lh)
        tab = sb("tab", [P, N_TABLES], scope=lh)
        lh.close()
        le.close()
        lf = ExitStack()
        sq = sb("sq", [P, D], scope=lf)
        r_one = sb("r_one", [P, 4], scope=lf)
        xr = sb("xr", [P, D], scope=lf)
        xrT = sb("xrT", [P, KD, T], scope=lf)
        rot = sb("rot", [P, 3, 2 * D], scope=lf)
        qkT = sb("qkT", [P, 4, T], scope=lf)
        k_blocks = sb("k_blocks", [P, KD, 8, T], scope=lf)
        v1 = sb("v1", [P, D], scope=lf)
        scoreT = sb("scoreT", [P, H, T], scope=lf)
        ffT = sb("ffT", [P, CT, T], scope=lf)
        y = sb("y", [P, D], scope=lf)
        y2 = sb("y2", [P, D], scope=lf)
        gn = sb("gn", [P, 3, H], scope=lf)
        gate1 = sb("gate1", [P, D], scope=lf)
        yT = sb("yT", [P, KD, T], scope=lf)
        pT = sb("pT", [64, T], scope=lf)
        hT = sb("hT", [P, FH // P, T], scope=lf)
        qT2 = sb("qT2", [64, T], scope=lf)
        lf.close()

        v_hist = {name: part(hw, HIST_COLS, name) for name in HIST_COLS}
        w_raw = part(hw, HIST_COLS, "W", KD)
        w1_hist = part(hw, HIST_COLS, "W1", CT)

        ld_const, ld_hist, ld_small = sem("ld_const"), sem("ld_hist"), sem("ld_small")
        ld_l0, ld_mask, ld_l1 = sem("ld_l0"), sem("ld_mask"), sem("ld_l1")
        ld_xw, ld_xo = sem("ld_xw"), sem("ld_xo")
        stored = sem("stored")
        dve_own, act_own, pool_own = sem("dve_own"), sem("act_own"), sem("pool_own")
        pe_s = Steps(sem("pe_steps"), PE_STEPS)
        dve_s = Steps(sem("dve_steps"), DVE_STEPS)
        act_s = Steps(sem("act_steps"), ACT_STEPS)
        pool_s = Steps(sem("pool_steps"), POOL_STEPS)
        h_loaded = [sem("h_loaded0"), sem("h_loaded1")]
        h_high, h_low, h_proj, h_sq = sem("h_high"), sem("h_low"), sem("h_proj"), sem("h_sq")
        h_add2, h_add1, h_ms, h_ve, h_rs, h_dg = (sem("h_add2"), sem("h_add1"), sem("h_ms"), sem("h_ve"), sem("h_rs"),
                                                  sem("h_dg"))
        h_bc, h_rw, h_nm, h_eh = sem("h_bc"), sem("h_rw"), sem("h_nm"), sem("h_eh")
        h_w1, h_hid, h_w2, h_lg = sem("h_w1"), sem("h_hid"), sem("h_w2"), sem("h_lg")
        h_gm, h_p, h_ws, h_st = sem("h_gm"), sem("h_p"), sem("h_ws"), sem("h_st")
        c_loaded, c_high, c_low = sem("c_loaded"), sem("c_high"), sem("c_low")
        c_proj, c_kh, c_kl = sem("c_proj"), sem("c_kh"), sem("c_kl")
        c_stack = [[sem(f"c_stack{b}{q}") for q in range(4)] for b in range(2)]
        c_max, c_red = sem("c_max"), sem("c_red")
        c_vt, c_val = sem("c_vt"), sem("c_val")
        c_new, c_nt, c_ntc = sem("c_new"), sem("c_nt"), sem("c_ntc")
        c_al, c_alx, c_rs, c_hm = sem("c_al"), sem("c_alx"), sem("c_rs"), sem("c_hm")
        c_a1 = sem("c_a1")
        c_q = [sem("c_q0"), sem("c_q1")]
        c_sc, c_exp = sem("c_sc"), sem("c_exp")
        c_wt, c_ev = sem("c_wt"), sem("c_ev")
        gates_passed = sem("gates_passed")
        c_ot, c_add = sem("c_ot"), sem("c_add")

        block = outer.enter_context(nc.Block())

        @block.sync
        def _(sp):
            sp.dma_start(const[:, :], const_in).then_inc(ld_const, 16)
            sp.dma_start(hw[:, :], hist_in).then_inc(ld_hist, 16)
            hist_src = ctx_t.rearrange("(k p) s -> p k s", p=P)

            def load_chunk(n, b):
                wait_at(sp, h_low, n - 1)
                sp.dma_start(hc_raw[:, b], hist_src[:, :, bass.ds(n * CH, CH)]).then_inc(h_loaded[b], 16)

            for n in range(8):
                load_chunk(n, n % 2)
            sp.dma_start(x[:, :], x_in).then_inc(ld_small, 16)
            sp.dma_start(rows0[:, :], rows0_in).then_inc(ld_small, 16)
            with sp.Fori(0, NCH // 8 - 1) as i:
                for r in range(8):
                    load_chunk(8 * i + (8 + r), r % 2)
                    piece = bass.ds((8 * i + r) * L0_PIECE, L0_PIECE)
                    sp.dma_start(w_l0[:, piece], l0_in[:, piece]).then_inc(ld_l0, 16)
            dve_s.wait(sp, "history_done")
            sp.dma_start(mask_bytes[:, :], mask_in).then_inc(ld_mask, 16)
            dve_s.wait(sp, "x1")
            sp.dma_start(x_wts[:, :], xw_in).then_inc(ld_xw, 16)
            sp.dma_start(x_bo[:, :], x_bo_in).then_inc(ld_xw, 16)

            def load_ctx(j):
                wait_at(sp, c_high, j)
                wait_at(sp, c_low, j)
                sp.dma_start(s_raw[:, :, :], hist_src[:, :, bass.ds(j * SC, SC)]).then_inc(c_loaded, 16)

            for j in range(3):
                load_ctx(j)
            with sp.Fori(3, NJ) as j:
                load_ctx(j)
            sp.wait_ge(c_val, KT * NJ)
            sp.wait_ge(c_kl, 4 * NJ)
            for b in range(2):
                for q in range(4):
                    sp.wait_ge(c_stack[b][q], 48 * NJ // 2)
            sp.dma_start(w1[:, :], l1_in).then_inc(ld_l1, 16)
            sp.dma_start(rows1[:, :], rows1_in).then_inc(ld_l1, 16)
            sp.dma_start(v_w[:, :], v_in).then_inc(ld_l1, 16)
            sp.dma_start(x_o[:, :, :], x_o_in.rearrange("(k d) n -> d k n", d=HD)).then_inc(ld_xo, 16)
            sp.wait_ge(c_sc, PAIRS * (NJ - 1))
            sp.dma_start(tab[:, :], tables_in).then_inc(ld_l1, 16)
            dve_s.wait(sp, "x6")
            sp.dma_start(out, x[:, :]).then_inc(stored, 16)
            sp.wait_ge(stored, 16)

        @block.tensor
        def _(pe):
            def product(out_ap, pairs):
                for n, (lhs, rhs) in enumerate(pairs):
                    last = nc.tensor.matmul(out_ap, lhs, rhs, start=(n == 0), stop=(n == len(pairs) - 1))
                return last

            dve_s.wait(pe, "hist_constants")
            pe.wait_ge(ld_hist, 16)
            pe_s.done(product(bank[:, 4, 0:CT], [(inv_width[:, :], v_hist["b"])]), "bias_mean")
            dve_s.wait(pe, "hist_weights")

            def project(n, b, half):
                if half == 0:
                    wait_at(pe, h_low, n + 1)
                wait_at(pe, h_nm, CT * (n - 2) + 2 * half + 2)
                for c in (2 * half, 2 * half + 1):
                    cols = slice(c * P, (c + 1) * P)
                    last = product(bank[:, 2 * b + half, (c % 2) * CH:(c % 2 + 1) * CH],
                                   [(w[:, k, cols], v[:, b, k]) for k in range(KD)
                                    for w, v in ((w_high, hc_high), (w_low, hc_high), (w_high, hc_low))])
                last.then_inc(h_proj, 1)

            def mean_square(n):
                pe.wait_ge(h_add1, n + 1)
                wait_at(pe, h_ve, n)
                for s in range(2):
                    last = nc.tensor.matmul(bank[0:HB, 4, s:s + 1], square1[:, s * HB:(s + 1) * HB],
                                            inv_width[:, 0:1], start=True, stop=True)
                last.then_inc(h_ms, 1)

            def spread_rstd(n):
                pe.wait_ge(h_dg, n + 1)
                wait_at(pe, h_rw, n)
                for s in range(2):
                    last = nc.tensor.matmul(bank[:, 5, s * HB:(s + 1) * HB], all_ones[0:HB, :], h_diag[:, s, :],
                                            start=True, stop=True)
                last.then_inc(h_bc, 1)

            def weight_hidden(n, gb, k):
                pe.wait_ge(h_eh, CT * n + CT)
                wait_at(pe, h_hid, n)
                product(bank[:, 6, 0:CH], [(w1_hist[:, c, :], eh[:, gb, c, k * CH:(k + 1) * CH])
                                           for c in range(CT)]).then_inc(h_w1, 1)

            def weight_logit(n):
                pe.wait_ge(h_hid, n + 1)
                wait_at(pe, h_lg, n)
                nc.tensor.matmul(bank[:, 7, 0:CH], w2_wide[:, :], hidden[:, :], start=True, stop=True).then_inc(h_w2, 1)

            def history_slot(n, s, last=NCH - 1):
                def here(lag):
                    return not isinstance(n, int) or 0 <= n - lag <= last
                if here(0):
                    project(n, s % 2, 0)
                if here(1):
                    mean_square(n - 1)
                if here(0):
                    project(n, s % 2, 1)
                if here(3):
                    weight_logit(n - 3)
                if here(1):
                    spread_rstd(n - 1)
                if here(2):
                    weight_hidden(n - 2, (s - 2) % 8 // GC, (s - 2) % GC)

            for n in range(8):
                history_slot(n, n)
            with pe.Fori(0, NCH // 8 - 1) as i:
                for r in range(8):
                    history_slot(8 * i + (8 + r), r)
            for n in range(NCH, NCH + 4):
                history_slot(n, n % 8)

            def turn(name_in, src, name_out, at=0, banks=None):
                dve_s.wait(pe, name_in)
                for k in range(KD):
                    last = nc.tensor.transpose(bank[:, at, k * P:(k + 1) * P], src[:, k * P:(k + 1) * P], ident)
                pe_s.done(last, name_out)

            def bias(rows, cols, name, lo=0, width=None):
                at, n = cols[name]
                width = n if width is None else width
                return (ones_row[0:1, :], rows[0:1, at + lo:at + lo + width])

            pe.wait_ge(ld_small, 32)
            pe.wait_ge(ld_l0, 16 * L0_PIECES)
            turn("xn1", xn, "xn1_t")
            dve_s.wait(pe, "xT1")
            wq, wk, wv = (part(w0, L0_COLS, n, KD) for n in ("x_q", "x_k", "x_v"))
            for m in range(KD):
                product(bank[:, 1, m * T:(m + 1) * T], [(wq[:, k, m * P:(m + 1) * P], xT[:, k]) for k in range(KD)])
                product(bank[:, 2, m * T:(m + 1) * T], [(wk[:, k, m * P:(m + 1) * P], xT[:, k]) for k in range(KD)])
            pe_s.done(product(bank[:, 3, 0:D], [(xT[:, k], wv[:, k]) for k in range(KD)]), "qkv0")
            dve_s.wait(pe, "q_blocks0")
            act_s.wait(pe, "kv0")
            for h in range(H):
                last = nc.tensor.matmul(bank[:, 4 + h // 4, (h % 4) * T:(h % 4 + 1) * T], q_blocks[:, h // 8, h % 8],
                                        kT[:, h // 8], start=True, stop=True)
                if h % 4 == 3:
                    pe_s.done(last, f"scores0_{h // 4}")
            for n, name in ((0, "shift_down"), (1, "shift_up")):
                for b in range(4):
                    dve_s.wait(pe, f"att0_{b}")
                    if n == 1:
                        act_s.wait(pe, f"down0_{b}")
                    pe_s.done(nc.tensor.matmul(bank[:, b, :], part(const, CONST_COLS, name),
                                               att[:, 1, 4 * b:4 * b + 4, 1:T + 1], start=True, stop=True),
                              f"{name}{b}")

            dve_s.wait(pe, "cc_wide")
            kg1, kg2 = part(w0, L0_COLS, "kg1", CT), part(w0, L0_COLS, "kg2", KD)
            pe_s.done(product(bank[:, 4, 0:D], [(cc_wide[:, c], kg1[:, c]) for c in range(CT)]
                              + [bias(rows0, L0_ROWS, "kg_b1")]), "kg1")
            act_s.wait(pe, "kg_h")
            for k in range(KD):
                last = nc.tensor.transpose(bank[:, 5, k * P:(k + 1) * P], kg_h[:, k * P:(k + 1) * P], ident)
            pe_s.done(last, "kg_t")
            dve_s.wait(pe, "kg_hT")
            pe_s.done(product(bank[:, 6, 0:H * 9], [(kg_hT[:, k], kg2[:, k]) for k in range(KD)]
                              + [bias(rows0, L0_ROWS, "kg_b2")]), "kg2")
            for h in range(H):
                if h % 4 == 0:
                    act_s.wait(pe, f"prob0_{h // 4}")
                last = nc.tensor.transpose(bank[:, h // 4, (h % 4) * T:(h % 4 + 1) * T], conv[:, h, :], ident)
                if h % 4 == 3:
                    pe_s.done(last, f"prob_t{h // 4}")
            for h in range(H):
                if h % 4 == 0:
                    dve_s.wait(pe, f"probT{h // 4}")
                last = nc.tensor.matmul(bank[:, 7, h * HD:(h + 1) * HD], probT[:, h, :], v0[:, h * HD:(h + 1) * HD],
                                        start=True, stop=True)
            pe_s.done(last, "pv0")
            turn("o0", o0, "o0_t")
            dve_s.wait(pe, "o0T")
            wo = part(w0, L0_COLS, "x_proj", KD)
            pe_s.done(product(bank[:, 1, 0:D], [(oT[:, k], wo[:, k]) for k in range(KD)]
                              + [bias(rows0, L0_ROWS, "proj_b")]), "proj0")

            turn("xn2", xn, "xn2_t")
            dve_s.wait(pe, "xT2")
            kvh, aq, ao = part(w0, L0_COLS, "a_kvh", KD), part(w0, L0_COLS, "a_q", KD), part(w0, L0_COLS, "a_o", KD)
            product(bank[:, 2, :], [(xT[:, k], kvh[:, k, 0:2 * D]) for k in range(KD)]
                    + [bias(rows0, L0_ROWS, "a_kvh", 0, 2 * D)])
            product(bank[:, 3, 0:D], [(xT[:, k], kvh[:, k, 2 * D:3 * D]) for k in range(KD)]
                    + [bias(rows0, L0_ROWS, "a_kvh", 2 * D, D)])
            for m in range(KD):
                last = product(bank[:, 4, m * T:(m + 1) * T],
                               [(aq[:, k, m * P:(m + 1) * P], xT[:, k]) for k in range(KD)])
            pe_s.done(last, "qkvh1")
            act_s.wait(pe, "kq1")
            dve_s.wait(pe, "v1")
            for m in range(KD):
                nc.tensor.matmul(bank[:, 5, m * P:(m + 1) * P], k_sig[:, m * P:(m + 1) * P], v_lin[:, m * P:(m + 1) * P],
                                 start=True, stop=True)
            for m in range(KD):
                last = nc.tensor.matmul(bank[:, 6, m:m + 1], k_sig[:, m * P:(m + 1) * P], ones[:, :],
                                        start=True, stop=True)
            pe_s.done(last, "kv1")
            dve_s.wait(pe, "kv_blocks")
            for m in range(KD):
                nc.tensor.matmul(bank[:, 0, m * P:(m + 1) * P], q_sig[:, m], kv[:, m], start=True, stop=True)
                last = nc.tensor.matmul(bank[:, 1, m * P:(m + 1) * P], q_sig[:, m], k_sum[:, m], start=True, stop=True)
            pe_s.done(last, "num_den")
            turn("gated1", att1, "gated1_t", at=7)
            dve_s.wait(pe, "gT")
            pe_s.done(product(bank[:, 2, 0:D], [(gT[:, k], ao[:, k]) for k in range(KD)]
                              + [bias(rows0, L0_ROWS, "a_bo")]), "proj1")

            turn("xn3", xn, "xn3_t")
            dve_s.wait(pe, "xT3")
            wg = part(w0, L0_COLS, "gates", KD)
            pe_s.done(product(bank[:, 1, 0:E + 1], [(xT[:, k], wg[:, k]) for k in range(KD)]), "gates")
            gate, up = part(wf, FFN_COLS, "gate", KD), part(wf, FFN_COLS, "up", KD)
            sgate, sup = part(wf, FFN_COLS, "s_gate", KD), part(wf, FFN_COLS, "s_up", KD)
            down, sdown = part(wf, FFN_COLS, "down", E), part(wf, FFN_COLS, "s_down", 4)

            def keys_product(j, b, u, at=7):
                m, w = divmod(u, 2)
                if u == 0:
                    pe.wait_ge(c_high, j + 1)
                    pe.wait_ge(c_low, j + 1)
                product(bank[:, at, 0:SW],
                        [(ww[:, k, m * P:(m + 1) * P], v[:, k, w * SW:(w + 1) * SW]) for k in range(KD)
                         for ww, v in ((x_high, s_high), (x_low, s_high), (x_high, s_low))]).then_inc(c_proj, 1)

            def expand(r):
                if r >= 2:
                    dve_s.wait(pe, f"hid{r - 2}")
                for n in range(ER):
                    wa, wb, c = (gate, up, r * ER + n) if r < E // ER else (sgate, sup, n)
                    product(bank[:, 2 + 2 * (r % 2), n * T:(n + 1) * T],
                            [(wa[:, k, c * P:(c + 1) * P], xT[:, k]) for k in range(KD)])
                    last = product(bank[:, 3 + 2 * (r % 2), n * T:(n + 1) * T],
                                   [(wb[:, k, c * P:(c + 1) * P], xT[:, k]) for k in range(KD)])
                pe_s.done(last, f"expand{r}")

            def contract(r):
                dve_s.wait(pe, f"hid{r}")
                if r >= 1:
                    dve_s.wait(pe, f"mixed{r - 1}")
                if r < E // ER:
                    for n in range(ER):
                        last = nc.tensor.matmul(bank[:, 6 + n // 2, (n % 2) * D:(n % 2 + 1) * D], hid[:, r % 2, n],
                                                down[:, r * ER + n], start=True, stop=True)
                else:
                    last = product(bank[:, 6, 0:D], [(hid[:, r % 2, n], sdown[:, n]) for n in range(4)])
                pe_s.done(last, f"contract{r}")

            ROUNDS = E // ER + 1
            expand(0)
            for r in range(1, ROUNDS):
                expand(r)
                for u in range(2 * r - 2, 2 * r):
                    if r == 1:
                        dve_s.wait(pe, "g_neg")
                    else:
                        pe.wait_ge(c_kh, u - 1)
                        pe.wait_ge(c_kl, u - 1)
                    keys_product(u // 4, u // 4, u % 4, at=u % 2)
                contract(r - 1)
            contract(ROUNDS - 1)

            pe.wait_ge(c_kh, 8)
            pe.wait_ge(c_kl, 8)
            turn("xn4", xn, "xn4_t")
            pe.wait_ge(ld_xw, 32)
            dve_s.wait(pe, "xT4")
            xw = part(x_wts, XW_COLS, "x_w", KD)
            for m in range(KD):
                last = product(bank[:, 1, m * T:(m + 1) * T],
                               [(xw[:, k, m * P:(m + 1) * P], xT[:, k]) for k in range(KD)])
            pe_s.done(last, "q4")
            dve_s.wait(pe, "q4_parts")
            for q in range(4):
                last = product(bank[:, 2 + q // 2, (q % 2) * 2 * T:(q % 2 + 1) * 2 * T],
                               [(part(const, CONST_COLS, "sel_high")[:, q * P:(q + 1) * P], q_h[:, :, :].bitcast(F32)),
                                (part(const, CONST_COLS, "sel_low")[:, q * P:(q + 1) * P], q_l[:, :, :])])
            pe_s.done(last, "q4_stack")

            dve_s.wait(pe, "q_base")

            def value_tile(j, b, k):
                pe.wait_ge(c_kl, 4 * j + 4)
                pe.wait_ge(c_kh, 4 * j + 4)
                out4 = bank[:, 7, 0:D].rearrange("p (q m c) -> p q m c", q=4, m=KD)
                for m in range(KD):
                    last = product(out4[:, :, m, :],
                                   [(kk[:, b, m, k * P:(k + 1) * P], ident_r[:, :]) for kk in (k_high, k_low)])
                last.then_inc(c_vt, 1)

            def turn_maxima(j, b):
                pe.wait_ge(c_new, j + 1)
                nc.tensor.transpose(bank[0:H, 7, 0:T], neg_max[:, b, :].bitcast(F32), ident).then_inc(c_nt, 1)

            def turn_sums(j, half):
                pe.wait_ge(c_ev, NG * j + 4 * half + 4)
                for g in range(4 * half, 4 * half + 4):
                    last = nc.tensor.transpose(bank[:, 7, (g % 4) * P:(g % 4 + 1) * P], o_part[:, g, :], ident)
                last.then_inc(c_ot, 1)

            def keys_read(j, u):
                return lambda: (pe.wait_ge(c_kh, 4 * j + u + 1), pe.wait_ge(c_kl, 4 * j + u + 1))

            def values_read(j, k):
                return lambda: pe.wait_ge(c_val, KT * j + k + 1)

            def maxima_read(j):
                return lambda: pe.wait_ge(c_ntc, j + 1)

            def sums_read(j, half):
                return lambda: pe.wait_ge(c_add, 2 * j + half + 1)

            def maximum_unit(j, b, n, v):
                h, w = divmod(v, 2)
                g, hh = divmod(h, 2)
                if v % 8 == 0:
                    pe.wait_ge(c_stack[b][v // 8], 48 * (n + 1))
                wait_at(pe, c_red, 2 * H * j + bank_free(MAX_BANKS, 2 * H, v))
                nc.tensor.matmul(bank[:, bank_of(MAX_BANKS, v), 0:SW], q_base[0:ONE_ROW, g, hh * T:(hh + 1) * T],
                                 k_stack[b][0:ONE_ROW, g, w * SW:(w + 1) * SW], start=True, stop=True).then_inc(c_max, 1)

            def scores(j, b, p):
                wait_at(pe, c_exp, PAIRS * j + bank_free(EXP_BANKS, PAIRS, p))
                for u in (2 * p, 2 * p + 1):
                    g, k = divmod(u, KT)
                    last = nc.tensor.matmul(bank[:, bank_of(EXP_BANKS, p), (u % 2) * 2 * T:(u % 2 + 1) * 2 * T],
                                            k_stack[b][0:STACK, g, k * P:(k + 1) * P], q_stack[0:STACK, b, g, :],
                                            start=True, stop=True)
                last.then_inc(c_sc, 1)

            def weigh(j, b, p):
                pe.wait_ge(c_exp, PAIRS * j + p + 1)
                if p == 0:
                    pe.wait_ge(c_val, KT * j + KT)
                for u in (2 * p, 2 * p + 1):
                    g, k = divmod(u, KT)
                    if k == 0:
                        wait_at(pe, c_ev, NG * j + g - 1)
                    for hh in range(2):
                        at = 32 * (2 * hh + k % 2)
                        v_at = (k * H + 2 * g + hh) * VW
                        last = nc.tensor.matmul(bank[at:at + 32, 2 + g % 2, 0:T],
                                                vals[:, b, v_at:v_at + 32],
                                                prob[:, p % NPB, u % 2, hh * T:(hh + 1) * T],
                                                start=(k < 2), stop=(k >= KT - 2))
                last.then_inc(c_wt, 1)

            def context_slot(n, b, first=False, more=True, build=True):
                j = 2 * n + b
                free = maxima_read(j)
                for p in range(PAIRS):
                    if more:
                        for v in LATE_UNITS[p]:
                            maximum_unit(j + 1, 1 - b, n + b, v)
                    if build:
                        for v in EARLY_UNITS[p]:
                            maximum_unit(j + 2, b, n + 1, v)
                    if p == 0:
                        pe.wait_ge(c_q[b], 16 * (n + 1))
                    scores(j, b, p)
                    if p >= PV_LAG:
                        weigh(j, b, p - PV_LAG)
                    elif not first:
                        weigh(j - 1, 1 - b, PAIRS - PV_LAG + p)
                    if build and p in KEY_AT:
                        u = KEY_AT.index(p)
                        free()
                        keys_product(j + 2, b, u)
                        free = keys_read(j + 2, u)
                    if p == SUM1_AT and not first:
                        free()
                        turn_sums(j - 1, 1)
                        free = sums_read(j - 1, 1)
                    if more and p in VAL_AT:
                        free()
                        value_tile(j + 1, 1 - b, VAL_AT.index(p))
                        free = values_read(j + 1, VAL_AT.index(p))
                    if p == SUM0_AT:
                        free()
                        turn_sums(j, 0)
                        free = sums_read(j, 0)
                    if more and p == MAX_AT:
                        free()
                        turn_maxima(j + 1, 1 - b)
                return free

            free = lambda: None
            for k in range(KT):
                free()
                value_tile(0, 0, k)
                free = values_read(0, k)
            for v in range(2 * H):
                maximum_unit(0, 0, 0, v)
            free()
            turn_maxima(0, 0)
            for v in range(EARLY):
                maximum_unit(1, 1, 0, v)
            context_slot(0, 0, first=True)
            context_slot(0, 1)
            with pe.Fori(1, NJ // 2 - 1) as i:
                for b in range(2):
                    context_slot(i, b)
            context_slot(NJ // 2 - 1, 0, build=False)
            free = context_slot(NJ // 2 - 1, 1, build=False, more=False)
            for p in range(PAIRS - PV_LAG, PAIRS):
                weigh(NJ - 1, 1, p)
            free()
            turn_sums(NJ - 1, 1)
            dve_s.wait(pe, "o1")
            for h in range(H):
                last = nc.tensor.transpose(bank[0:HD, h // 4, (h % 4) * T:(h % 4 + 1) * T], o1[:, h * HD:(h + 1) * HD],
                                           ident)
            pe_s.done(last, "o1_t")
            dve_s.wait(pe, "o1T")
            pe.wait_ge(ld_xo, 16)
            pe_s.done(product(bank[:, 1, 0:D], [(o1T[:, k::ROW_TOKENS], x_o[:, k, :]) for k in range(ROW_TOKENS)]
                              + [(ones_row[:, :], x_bo[:, :])]), "proj4")

            turn("xn5", xn, "xn5_t")
            pe.wait_ge(ld_l1, 64)
            dve_s.wait(pe, "xT5")
            qkv, ff, gated, wp = (part(w1, L1_COLS, n, KD) for n in ("qkv", "ff", "gated", "proj"))
            wff = part(w1, L1_COLS, "w_ff", CT)
            dve_s.wait(pe, "xr")
            for k in range(KD):
                last = nc.tensor.transpose(bank[:, 1, k * P:(k + 1) * P], xr[:, k * P:(k + 1) * P], ident)
            pe_s.done(last, "xr_t")
            pe_s.done(product(bank[:, 2, 0:D], [(xT[:, k], gated[:, k]) for k in range(KD)]
                              + [bias(rows1, L1_ROWS, "b_gated")]), "gated5")
            dve_s.wait(pe, "xrT")
            product(bank[:, 3, :], [(xrT[:, k], qkv[:, k, 0:2 * D]) for k in range(KD)])
            pe_s.done(product(bank[:, 4, 0:D], [(xrT[:, k], qkv[:, k, 2 * D:3 * D]) for k in range(KD)]), "qkv5")
            for c in range(CT):
                last = product(bank[:, 5, c * T:(c + 1) * T],
                               [(ff[:, k, c * P:(c + 1) * P], xrT[:, k]) for k in range(KD)])
            pe_s.done(last, "ff5")
            dve_s.wait(pe, "rot")
            for n in range(4):
                last = nc.tensor.transpose(bank[:, 6, n * T:(n + 1) * T], rot[:, 0, n * P:(n + 1) * P], ident)
            pe_s.done(last, "rot_t")
            dve_s.wait(pe, "k_blocks5")
            for h in range(H):
                if h == 0:
                    act_s.wait(pe, "ffT")
                last = nc.tensor.matmul(bank[:, SCORE_BANKS[h // 4], (h % 4) * T:(h % 4 + 1) * T],
                                        k_blocks[:, h // 8, h % 8], qkT[:, h // 8], start=True, stop=True)
                if h % 4 == 3:
                    pe_s.done(last, f"scores5_{h // 4}")
            for h in range(H):
                if h % 4 == 0:
                    dve_s.wait(pe, f"scoreT{h // 4}")
                last = nc.tensor.matmul(bank[:, 6, h * HD:(h + 1) * HD], scoreT[:, h, :], v1[:, h * HD:(h + 1) * HD],
                                        start=True, stop=True)
            pe_s.done(last, "y5")
            turn("y5n", y, "y5_t")
            dve_s.wait(pe, "yT")
            pe_s.done(product(bank[:, 1, 0:D], [(yT[:, k], wp[:, k]) for k in range(KD)]
                              + [(ffT[:, c], wff[:, c]) for c in range(CT)]
                              + [bias(rows1, L1_ROWS, "b_proj")]), "proj5")

            turn("xn6", xn, "xn6_t")
            dve_s.wait(pe, "xT6")
            u1, u2 = part(w1, L1_COLS, "u1", KD), part(w1, L1_COLS, "u2", FH // P)
            v1w, v2w = part(v_w, V_COLS, "v1"), part(v_w, V_COLS, "v2")
            pe_s.done(product(bank[0:64, 1, 0:T], [(u1[:, k], xT[:, k]) for k in range(KD)]), "p6")
            dve_s.wait(pe, "pT")
            for c in range(FH // P):
                last = nc.tensor.matmul(bank[:, 2 + c // 4, (c % 4) * T:(c % 4 + 1) * T], v1w[:, c * P:(c + 1) * P],
                                        pT[:, :], start=True, stop=True)
            pe_s.done(last, "h6")
            act_s.wait(pe, "hT")
            pe_s.done(product(bank[0:64, 4, 0:T], [(u2[:, c], hT[:, c]) for c in range(FH // P)]), "q6")
            dve_s.wait(pe, "qT2")
            pe_s.done(product(bank[:, 5, 0:D], [(qT2[:, :], v2w), bias(rows1, L1_ROWS, "b2")]), "out6")

        @block.scalar
        def _(act):
            own = [0]

            def link(ins):
                own[0] += 1
                ins.then_inc(act_own, 1)
                act.wait_ge(act_own, own[0])

            A = nc.scalar.activation
            act.wait_ge(ld_hist, 16)
            dve_s.wait(act, "hist_weights")

            def hide_act(n):
                act.wait_ge(h_w1, n + 1)
                wait_at(act, h_w2, n)
                A(hidden[:, :], bank[:, 6, 0:CH], ACT.Gelu, bias=v_hist["b1"]).then_inc(h_hid, 1)

            def features(n, gb, k, group):
                for c in range(CT):
                    if k == 0:
                        wait_at(act, h_ws, CT * (group - 2) + c + 1)
                    act.wait_ge(h_nm, CT * n + c + 1)
                    A(eh[:, gb, c, k * CH:(k + 1) * CH], normed[:, k % 2, c, :], ACT.Gelu,
                      bias=v_hist["beta"][:, c:c + 1], scale=v_hist["g"][:, c:c + 1]).then_inc(h_eh, 1)

            def squares(n, b):
                wait_at(act, h_add2, n)
                for c in range(CT):
                    if c % 2 == 0:
                        act.wait_ge(h_proj, 2 * n + c // 2 + 1)
                    ins = A(square[:, c, :], bank[:, 2 * b + c // 2, (c % 2) * CH:(c % 2 + 1) * CH], ACT.Square,
                            bias=b_centered[:, c:c + 1])
                ins.then_inc(h_sq, 1)

            def widen(n):
                act.wait_ge(h_bc, n + 1)
                wait_at(act, h_nm, CT * n)
                A(rstd_wide[:, :], bank[:, 5, 0:CH], ACT.Copy).then_inc(h_rw, 1)

            def weights(group, gb):
                act.wait_ge(h_gm, group + 1)
                wait_at(act, h_ws, CT * (group - 1))
                wait_at(act, h_st, group - 1)
                A(weight[:, gb, :], logits[:, gb, :], ACT.Exp, bias=stat[:, gb, 5:6],
                  accum_out=stat[:, gb, 4:5]).then_inc(h_p, 1)

            def history_slot(n, s, group, last=NCH - 1):
                def here(lag):
                    return not isinstance(n, int) or 0 <= n - lag <= last
                if here(3):
                    hide_act(n - 3)
                if here(2):
                    features(n - 2, (s - 2) % 8 // GC, (s - 2) % GC, group(s - 2))
                if s % GC == 3 and here(7):
                    weights(group(s - 7), (s - 7) % 8 // GC)
                if here(0):
                    squares(n, s % 2)
                if here(1):
                    widen(n - 1)

            for n in range(8):
                history_slot(n, n, lambda s: s // GC)
            with act.Fori(0, NCH // 8 - 1) as i:
                for r in range(8):
                    history_slot(8 * i + (8 + r), r, lambda s: 2 * i + (2 + s // GC))
            for n in range(NCH, NCH + 5):
                history_slot(n, n % 8, lambda s: NCH // GC + s // GC)

            pe_s.wait(act, "qkv0")
            dve_s.wait(act, "history_done")
            A(kT[:, :, :], bank[:, 2, 0:D].rearrange("p (m t) -> p m t", m=KD), ACT.Copy).then_inc(act_own, 1)
            own[0] += 1
            act_s.done(A(v0[:, :], bank[:, 3, 0:D], ACT.Copy), "kv0")
            for n, name in ((0, "shift_down"), (1, "shift_up")):
                for b in range(4):
                    pe_s.wait(act, f"{name}{b}")
                    act_s.done(A(att[:, 2 * n, 4 * b:4 * b + 4, 1:T + 1],
                                 bank[:, b, :].rearrange("p (h t) -> p h t", t=T), ACT.Copy),
                               ("down0_", "up0_")[n] + str(b))
            dve_s.wait(act, "g_shift")
            act_s.done(A(g_w[:, :], g_w[:, :], ACT.Exp), "g_w")
            dve_s.wait(act, "kg_n")
            act_s.done(A(kg_h[:, :], kg_n[:, :], ACT.Gelu), "kg_h")
            dve_s.wait(act, "kern_shift")
            act_s.done(A(kern[:, :, :], kern[:, :, :], ACT.Exp), "kern_e")
            dve_s.wait(act, "s_max")
            for h in range(H):
                if h == DVE_HEADS:
                    dve_s.wait(act, "s_max_rest")
                ins = A(conv[:, h, :], conv[:, h, :], ACT.Exp, bias=s_max[:, h:h + 1], accum_out=s_sum[:, h:h + 1])
                if h % 4 == 3:
                    act_s.done(ins, f"prob0_{h // 4}")

            pe_s.wait(act, "qkvh1")
            dve_s.wait(act, "xT2")
            link(A(k_sig[:, :], bank[:, 2, 0:D], ACT.Sigmoid))
            abq = part(w0, L0_COLS, "a_bq")
            link(A(q_sig[:, 0, :], bank[:, 4, 0:T], ACT.Sigmoid, bias=abq[:, 0:1]))
            act_s.done(A(q_sig[:, 1, :], bank[:, 4, T:2 * T], ACT.Sigmoid, bias=abq[:, 1:2]), "kq1")

            dve_s.wait(act, "g_neg")
            act_s.done(A(e_gate[:, :], e_log[:, 0:E], ACT.Exp, bias=g_neg[:, :]), "e_gate")
            act_s.done(A(s_gate[:, :], e_log[:, E:E + 1], ACT.Exp, scale=-1.0), "s_gate_e")
            xb = part(x_wts, XW_COLS, "x_b")

            def keys_high(j, b, n, u, at=7):
                m, w = divmod(u, 2)
                act.wait_ge(c_proj, 4 * j + u + 1)
                if u == 0:
                    for q in range(4):
                        wait_at(act, c_stack[b][q], 48 * n)
                A(k_high[:, b, m, w * SW:(w + 1) * SW], bank[:, at, 0:SW], ACT.Identity,
                  bias=xb[:, m:m + 1]).then_inc(c_kh, 1)

            for r in range(E // ER + 1):
                pe_s.wait(act, f"expand{r}")
                if r >= 2:
                    dve_s.wait(act, f"hid{r - 2}")
                act_s.done(A(silu[:, r % 2], bank[:, 2 + 2 * (r % 2), :].rearrange("p (n t) -> p n t", t=T), ACT.Silu),
                           f"silu{r}")
                if r == 1:
                    act.wait_ge(ld_xw, 32)
                if r >= 1:
                    for u in range(2 * r - 2, 2 * r):
                        keys_high(u // 4, u // 4, 0, u % 4, at=u % 2)

            def value_copy(j, b, k):
                act.wait_ge(c_vt, KT * j + k + 1)
                if k == 0:
                    wait_at(act, c_wt, PAIRS * (j - 1))
                    pool_s.wait(act, "c_zero")
                v = vals[:, b, k * H * VW:(k + 1) * H * VW].rearrange("p (h c) -> p h c", c=VW)[:, :, 0:HD]
                A(v, bank[:, 7, 0:D].rearrange("p (h c) -> p h c", c=HD), ACT.Copy).then_inc(c_val, 1)

            def exponentials(j, b, p):
                act.wait_ge(c_sc, PAIRS * j + p + 1)
                wait_at(act, c_wt, PAIRS * j + p - NPB + 1)
                A(prob[:, p % NPB, :, :], bank[:, bank_of(EXP_BANKS, p), :].rearrange("p (u t) -> p u t", u=2),
                  ACT.Exp).then_inc(c_exp, 1)

            def sums_copy(j, g):
                act.wait_ge(c_wt, PAIRS * j + (KT * g + KT - 1) // 2 + 1)
                wait_at(act, c_ot, 2 * (j - 1) + g // 4 + 1)
                A(o_part[:, g, :], bank[:, 2 + g % 2, 0:T], ACT.Copy).then_inc(c_ev, 1)

            def rescale(j):
                act.wait_ge(c_al, j + 1)
                wait_at(act, c_rs, j)
                A(alpha[:, :], alpha_log[:, :], ACT.Exp).then_inc(c_alx, 1)

            def context_slot(n, b, first=False, more=True, build=True):
                j = 2 * n + b
                for p in range(PAIRS):
                    exponentials(j, b, p)
                    if build and p in KEY_AT:
                        keys_high(j + 2, b, n + 1, KEY_AT.index(p))
                    if p == SUM1_AT:
                        rescale(j)
                    if more and p in VAL_AT:
                        value_copy(j + 1, 1 - b, VAL_AT.index(p))
                    for g in range(NG):
                        if GROUP_END[g] == p - PV_LAG:
                            sums_copy(j, g)
                        if not first and GROUP_END[g] == p - PV_LAG + PAIRS:
                            sums_copy(j - 1, g)

            for k in range(KT):
                value_copy(0, 0, k)
            context_slot(0, 0, first=True)
            context_slot(0, 1)
            with act.Fori(1, NJ // 2 - 1) as i:
                for b in range(2):
                    context_slot(i, b)
            context_slot(NJ // 2 - 1, 0, build=False)
            context_slot(NJ // 2 - 1, 1, build=False, more=False)
            sums_copy(NJ - 1, NG - 1)

            pe_s.wait(act, "ff5")
            act.wait_ge(ld_l1, 64)
            dve_s.wait(act, "xrT")
            act_s.done(A(ffT[:, :, :], bank[:, 5, :].rearrange("p (c t) -> p c t", t=T), ACT.Gelu), "ffT")
            act_s.done(A(gate1[:, :], bank[:, 2, 0:D], ACT.Silu), "gate1")

            pe_s.wait(act, "h6")
            b1 = part(w1, L1_COLS, "b1")
            for c in range(FH // P):
                ins = A(hT[:, c, :], bank[:, 2 + c // 4, (c % 4) * T:(c % 4 + 1) * T], ACT.Gelu_apprx_tanh,
                        bias=b1[:, c:c + 1])
            act_s.done(ins, "hT")

        @block.gpsimd
        def _(pool):
            TT = nc.gpsimd.tensor_tensor
            nc.gpsimd.memset(half_power[:, 0:1], -0.5).then_inc(pool_own, 1)
            pool_s.done(nc.gpsimd.memset(half_power[:, 1:2], 0.5), "half_power")
            pool.wait_ge(pool_own, 1)
            pool_s.wait(pool, "half_power")
            pool.wait_ge(ld_const, 16)

            def low_part(n, b):
                pool.wait_ge(h_high, n + 1)
                TT(hc_low[:, b], hc_raw[:, b], hc_high[:, b].bitcast(F32), ALU.subtract).then_inc(h_low, 1)

            def deviation(n):
                pool.wait_ge(h_ve, n + 1)
                TT(h_rstd[:, :], h_var[:, :], half_power[0:HB, 0:1].broadcast_to([HB, 2]), ALU.pow).then_inc(h_rs, 1)
                pool.wait_ge(h_rs, n + 1)
                wait_at(pool, h_bc, n)
                TT(h_diag[:, :, :], const[0:HB, 0:HB].unsqueeze(1).broadcast_to([HB, 2, HB]),
                   h_rstd[:, :].unsqueeze(2).broadcast_to([HB, 2, HB]), ALU.mult).then_inc(h_dg, 1)

            def history_slot(m, s, last=NCH - 1):
                if not isinstance(m, int) or 0 <= m - 2 <= last:
                    wait_at(pool, h_dg, m - 2)
                    deviation(m - 2)
                if not isinstance(m, int) or m <= last:
                    low_part(m, s % 2)

            for m in range(8):
                history_slot(m, m)
            with pool.Fori(0, NCH // 8 - 1) as i:
                for r in range(8):
                    history_slot(8 * i + (8 + r), r)
            for m in range(NCH, NCH + 2):
                history_slot(m, m % 8)

            def power(name_in, name_out, to, of, which=0):
                dve_s.wait(pool, name_in)
                n = of.shape[1]
                pool_s.done(TT(to, of, half_power[:, which:which + 1].broadcast_to([P, n]), ALU.pow), name_out)

            power("var1", "rstd1", rstd[:, :], var_eps[:, :])
            power("var_kg", "rstd_kg", rstd[:, :], var_eps[:, :])
            dve_s.wait(pool, "kernels")
            act_s.wait(pool, "up0_3")
            passed = [1]

            def link(ins):
                passed[0] += 1
                ins.then_inc(pool_own, 1)
                pool.wait_ge(pool_own, passed[0])

            rest = H - DVE_HEADS
            theirs = conv[:, DVE_HEADS:H, :]
            for tap in range(9):
                src = att[:, tap // 3, DVE_HEADS:H, tap % 3:tap % 3 + T]
                weight_of = kern[:, DVE_HEADS:H, tap:tap + 1].broadcast_to([P, rest, T])
                link(TT(theirs if tap == 0 else tap_part[:, :, :], src, weight_of, ALU.mult))
                if tap > 0:
                    link(TT(theirs, theirs, tap_part[:, :, :], ALU.add))
            link(TT(theirs, theirs, keep[:, :].unsqueeze(1).broadcast_to([P, rest, T]), ALU.mult))
            pool_s.done(TT(theirs, theirs, hide[:, :].unsqueeze(1).broadcast_to([P, rest, T]), ALU.add), "conv")
            power("var2", "rstd2", rstd[:, :], var_eps[:, :])
            power("var_att", "rstd_att", rstd[:, :], var_eps[:, :])
            def context_low(j):
                pool.wait_ge(c_high, j + 1)
                TT(s_low[:, :, :], s_raw[:, :, :], s_high[:, :, :].bitcast(F32), ALU.subtract).then_inc(c_low, 1)

            def gate(number):
                wait_at(pool, gates_passed, number)
                TT(gate_cell[:, :], half_power[0:1, 0:1], half_power[0:1, 0:1], ALU.mult).then_inc(gates_passed, 1)

            def stack(j, b, q, number):
                wait_at(pool, c_kh, 4 * j + 4)
                wait_at(pool, c_kl, 4 * j + 4)
                wait_at(pool, c_sc, PAIRS * (j - 2) + 7 * q + 7)
                gate(number)
                for n, src in enumerate((k_high, k_low, k_high)):
                    nc.gpsimd.dma_start(k_stack[b][32 * n:32 * n + 32, 2 * q:2 * q + 2, :],
                                        src[32 * q:32 * q + 32, b, :, :]).then_inc(c_stack[b][q], 16)

            def maxima(j, b, number):
                wait_at(pool, c_ntc, j + 1)
                wait_at(pool, c_sc, PAIRS * (j - 1))
                gate(number)
                nc.gpsimd.dma_start(q_stack[ONE_ROW:ONE_ROW + 1, b, :, :], neg_maxT[:, :]).then_inc(c_q[b], 16)

            def context_slot(j, b, ahead=True):
                for q in range(4):
                    if q == 2 and ahead:
                        context_low(j + 3)
                    if q == 3:
                        maxima(j + 1, 1 - b, 5 * j + 12)
                    stack(j + 2, b, q, 5 * j + 9 + q + q // 3)

            context_low(0)
            power("var3", "rstd3", rstd[:, :], var_eps[:, :])
            for q in range(4):
                stack(0, 0, q, q)
                if q == 0:
                    context_low(1)
            power("var4", "rstd4", rstd[:, :], var_eps[:, :])
            nc.gpsimd.memset(vals[:, :, :], 1.0).then_inc(pool_own, 1)
            pool_s.done(nc.gpsimd.memset(acc[:, :, :, :], 0.0), "c_zero")
            for q in range(4):
                stack(1, 1, q, 4 + q)
            context_low(2)
            maxima(0, 0, 8)
            context_slot(0, 0)
            context_slot(1, 1)
            with pool.Fori(1, NJ // 2 - 2) as i:
                context_slot(2 * i, 0)
                context_slot(2 * i + 1, 1)
            context_slot(NJ - 4, 0)
            context_slot(NJ - 3, 1, ahead=False)
            maxima(NJ - 1, 1, 5 * (NJ - 2) + 9)
            power("var5", "rstd5", rstd[:, :], var_eps[:, :])
            power("ss5", "rms5", r_one[:, 1:2], r_one[:, 0:1], 1)
            power("gn_var", "gn_rstd", gn[:, 2, :], gn[:, 1, :])
            power("var6", "rstd6", rstd[:, :], var_eps[:, :])

        @block.vector
        def _(dve):
            V = nc.vector
            own = [0]

            def link(ins):
                own[0] += 1
                ins.then_inc(dve_own, 1)
                dve.wait_ge(dve_own, own[0])

            def done(ins, name):
                dve_s.done(ins, name)
                dve_s.wait(dve, name)

            V.memset(ones_row[:, :], 1.0).then_inc(dve_own, 1)
            V.memset(ones[:, :], 1.0).then_inc(dve_own, 1)
            V.memset(all_ones[:, :], 1.0).then_inc(dve_own, 1)
            own[0] += 3
            done(V.memset(inv_width[:, :], 1.0 / C2), "hist_constants")
            dve.wait_ge(ld_hist, 16)
            link(V.tensor_reduce(w_mean[:, :], w_raw, AX_X, ALU.add))
            link(V.tensor_scalar(w_mean[:, :], w_mean[:, :], 1.0 / C2, None, ALU.mult))
            link(V.tensor_tensor(w_centered[:, :, :], w_raw, w_mean[:, :].unsqueeze(2).broadcast_to([P, KD, C2]),
                                 ALU.subtract))
            link(V.tensor_copy(w_high[:, :, :], w_centered[:, :, :]))
            link(V.tensor_tensor(w_low[:, :, :], w_centered[:, :, :], w_high[:, :, :].bitcast(F32), ALU.subtract))
            link(V.tensor_copy(w2_wide[:, :], v_hist["W2"].broadcast_to([P, P])))
            pe_s.wait(dve, "bias_mean")
            link(V.tensor_reduce(b_mean[:, :], bank[:, 4, 0:CT], AX_X, ALU.add))
            done(V.tensor_scalar(b_centered[:, :], v_hist["b"], b_mean[:, :], None, ALU.subtract), "hist_weights")

            def high_part(m, b):
                dve.wait_ge(h_loaded[b], h_round(m))
                wait_at(dve, h_proj, 2 * (m - 1))
                V.tensor_copy(hc_high[:, b], hc_raw[:, b]).then_inc(h_high, 1)

            def h_round(m):
                return 16 * (m // 2 + 1)

            def variance(n):
                dve.wait_ge(h_ms, n + 1)
                wait_at(dve, h_rs, n)
                V.tensor_scalar(h_var[:, :], bank[0:HB, 4, 0:2], LN_EPS, None, ALU.add).then_inc(h_ve, 1)

            def add_squares(n):
                dve.wait_ge(h_sq, n + 1)
                wait_at(dve, h_add1, n)
                V.tensor_tensor(square2[:, :, :], square[:, 0:2, :], square[:, 2:4, :], ALU.add).then_inc(h_add2, 1)
                dve.wait_ge(h_add2, n + 1)
                wait_at(dve, h_ms, n)
                V.tensor_tensor(square1[:, :], square2[:, 0, :], square2[:, 1, :], ALU.add).then_inc(h_add1, 1)

            def normalise(n, b, half):
                dve.wait_ge(h_rw, n + 1)
                for c in (2 * half, 2 * half + 1):
                    wait_at(dve, h_eh, CT * (n - 2) + c + 1)
                    V.scalar_tensor_tensor(out=normed[:, b, c, :],
                                           in0=bank[:, 2 * b + half, (c % 2) * CH:(c % 2 + 1) * CH],
                                           scalar=b_centered[:, c:c + 1], in1=rstd_wide[:, :],
                                           op0=ALU.add, op1=ALU.mult).then_inc(h_nm, 1)

            def logit(n, gb, k, group):
                dve.wait_ge(h_w2, n + 1)
                if k == 0:
                    wait_at(dve, h_p, group - 1)
                    wait_at(dve, h_gm, group - 1)
                V.tensor_scalar(logits[:, gb, k * CH:(k + 1) * CH], bank[:, 7, 0:CH], v_hist["b2"], None,
                                ALU.add).then_inc(h_lg, 1)
                if k == GC - 1:
                    dve.wait_ge(h_lg, n + 1)
                    wait_at(dve, h_st, group - 1)
                    V.tensor_reduce(stat[:, gb, 5:6], logits[:, gb, :], AX_X, ALU.max, negate=True).then_inc(h_gm, 1)

            def weighted_sum(group, gb, c):
                dve.wait_ge(h_p, group + 1)
                wait_at(dve, h_st, group - 1)
                V.tensor_tensor_reduce(eh[:, gb, c, :], eh[:, gb, c, :], weight[:, gb, :], 1.0, 0.0, ALU.mult, ALU.add,
                                       stat[:, gb, c:c + 1]).then_inc(h_ws, 1)

            def store_stats(group, gb):
                dve.wait_ge(h_ws, CT * group + CT)
                V.tensor_copy(group_stats[:, bass.ds(group, 1), :], stat[:, gb:gb + 1, :]).then_inc(h_st, 1)

            def history_slot(m, s, group, last=NCH - 1):
                def here(lag, hi=last):
                    return not isinstance(m, int) or 0 <= m - lag <= hi
                if here(2):
                    variance(m - 2)
                if here(0):
                    high_part(m, s % 2)
                for lag, cs in ((9, (0, 1)), (10, (2, 3))):
                    if (s - lag) % GC == 0 and here(lag):
                        for c in cs:
                            weighted_sum(group(s - lag), (s - lag) % 8 // GC, c)
                if (s - 12) % GC == 0 and here(12):
                    store_stats(group(s - 12), (s - 12) % 8 // GC)
                if here(4):
                    logit(m - 4, (s - 4) % 8 // GC, (s - 4) % GC, group(s - 4))
                if here(2):
                    normalise(m - 2, s % 2, 0)
                if here(1):
                    add_squares(m - 1)
                if here(2):
                    normalise(m - 2, s % 2, 1)

            for m in range(16):
                history_slot(m, m % 8, lambda s: m // 8 * 2 + s // GC)
            loop_round = [None]
            with dve.Fori(0, NCH // 8 - 2) as i:
                def h_round(m):
                    return 64 * i + loop_round[0]
                for r in range(8):
                    loop_round[0] = 16 * ((16 + r) // 2 + 1)
                    history_slot(8 * i + (16 + r), r, lambda s: 2 * i + (4 + s // GC))
            for m in range(NCH, NCH + 9):
                history_slot(m, m - NCH, lambda s: NCH // GC + s // GC)
            dve.wait_ge(h_st, NGR)
            dve.wait_ge(pe_s.sem, 1)
            done(V.memset(g_one[:, :], 0.0), "history_done")

            def layer_norm(n, src=None):
                src = x if src is None else src
                link(V.bn_stats(stats6[:, :], src))
                link(V.bn_aggr(mv[:, :], stats6[:, :]))
                done(V.tensor_scalar(var_eps[:, :], mv[:, 1:2], LN_EPS, None, ALU.add), f"var{n}")
                pool_s.wait(dve, f"rstd{n}")

            def norm_turn(n):
                layer_norm(n, x[:, :])
                done(V.tensor_scalar(xn[:, :], x[:, :], mv[:, 0:1], rstd[:, :], ALU.subtract, ALU.mult), f"xn{n}")
                pe_s.wait(dve, f"xn{n}_t")
                done(V.tensor_copy(xT[:, :, :], turned(0)), f"xT{n}")

            def turned(b):
                return bank[:, b, 0:D].rearrange("p (k t) -> p k t", k=KD)

            dve.wait_ge(ld_small, 32)
            norm_turn(1)
            dve.wait_ge(ld_mask, 16)
            dve.wait_ge(ld_const, 16)
            link(V.tensor_copy(masked[:, :], mask_bytes[:, :].bitcast(U8)))
            link(V.tensor_scalar(keep[:, :], masked[:, :], -1.0, 1.0, ALU.mult, ALU.add))
            link(V.tensor_scalar(hide[:, :], masked[:, :], NEG, None, ALU.mult))
            link(V.memset(att[:, :, :, 0:1], 0.0))
            link(V.memset(att[:, :, :, T + 1:T + 2], 0.0))
            pe_s.wait(dve, "qkv0")

            def head_blocks(out, b, m, name=None):
                ins = V.tensor_tensor(out[:, m], b.unsqueeze(1).broadcast_to([P, 8, T]),
                                      head_col.unsqueeze(2).broadcast_to([P, 8, T]), ALU.mult)
                link(ins) if name is None else done(ins, name)

            head_blocks(q_blocks, bank[:, 1, 0:T], 0)
            head_blocks(q_blocks, bank[:, 1, T:2 * T], 1, "q_blocks0")
            for b in range(4):
                pe_s.wait(dve, f"scores0_{b}")
                done(V.scalar_tensor_tensor(out=att[:, 1, 4 * b:4 * b + 4, 1:T + 1],
                                            in0=bank[:, 4 + b, :].rearrange("p (h t) -> p h t", t=T), scalar=HD ** -0.5,
                                            in1=keep[:, :].unsqueeze(1).broadcast_to([P, 4, T]),
                                            op0=ALU.mult, op1=ALU.mult), f"att0_{b}")
            gs = group_stats
            link(V.tensor_reduce(g_max[:, :], gs[:, :, 5], AX_X, ALU.min))
            done(V.tensor_scalar(g_w[:, :], gs[:, :, 5], g_max[:, :], -1.0, ALU.subtract, ALU.mult), "g_shift")
            act_s.wait(dve, "g_w")
            link(V.tensor_tensor(g_sum[:, :], g_w[:, :], gs[:, :, 4], ALU.mult))
            link(V.tensor_reduce(g_one[:, :], g_sum[:, :], AX_X, ALU.add))
            link(V.reciprocal(g_one[:, :], g_one[:, :]))
            link(V.tensor_tensor(g_cc[:, :, :], gs[:, :, 0:CT], g_w[:, :].unsqueeze(2).broadcast_to([P, NGR, CT]),
                                 ALU.mult))
            link(V.tensor_reduce(cc[:, :], g_cc[:, :, :].rearrange("p g c -> p c g"), AX_X, ALU.add))
            link(V.tensor_scalar(cc[:, :], cc[:, :], g_one[:, :], None, ALU.mult))
            done(V.tensor_copy(cc_wide[:, :, :], cc[:, :].unsqueeze(2).broadcast_to([P, CT, P])), "cc_wide")
            pe_s.wait(dve, "kg1")
            layer_norm("_kg", bank[:, 4, 0:D])
            link(V.tensor_scalar(kg_n[:, :], bank[:, 4, 0:D], mv[:, 0:1], rstd[:, :], ALU.subtract, ALU.mult))
            link(V.tensor_tensor(kg_n[:, :], kg_n[:, :], part(w0, L0_COLS, "kg_g"), ALU.mult))
            done(V.tensor_tensor(kg_n[:, :], kg_n[:, :], part(w0, L0_COLS, "kg_b"), ALU.add), "kg_n")
            pe_s.wait(dve, "kg_t")
            done(V.tensor_copy(kg_hT[:, :, :], turned(5)), "kg_hT")
            pe_s.wait(dve, "kg2")
            kp = bank[:, 6, 0:H * 9].rearrange("p (h n) -> p h n", n=9)
            link(V.tensor_reduce(kern_m[:, :], kp, AX_X, ALU.max))
            done(V.tensor_tensor(kern[:, :, :], kp, kern_m[:, :].unsqueeze(2).broadcast_to([P, H, 9]), ALU.subtract),
                 "kern_shift")
            act_s.wait(dve, "kern_e")
            link(V.tensor_reduce(kern_m[:, :], kern[:, :, :], AX_X, ALU.add))
            link(V.reciprocal(kern_m[:, :], kern_m[:, :]))
            done(V.tensor_tensor(kern[:, :, :], kern[:, :, :], kern_m[:, :].unsqueeze(2).broadcast_to([P, H, 9]),
                                 ALU.mult), "kernels")
            act_s.wait(dve, "up0_3")
            for tap in range(9):
                for h in range(DVE_HEADS):
                    src = att[:, tap // 3, h, tap % 3:tap % 3 + T]
                    if tap == 0:
                        ins = V.tensor_scalar(conv[:, h, :], src, kern[:, h, 0:1], None, ALU.mult)
                    else:
                        dve.wait_ge(dve_own, own[0] - DVE_HEADS + 1)
                        ins = V.scalar_tensor_tensor(out=conv[:, h, :], in0=src, scalar=kern[:, h, tap:tap + 1],
                                                     in1=conv[:, h, :], op0=ALU.mult, op1=ALU.add)
                    ins.then_inc(dve_own, 1)
                    own[0] += 1
            dve.wait_ge(dve_own, own[0])
            wide = lambda a: a[:, :].unsqueeze(1).broadcast_to([P, DVE_HEADS, T])
            mine = conv[:, 0:DVE_HEADS, :]
            link(V.tensor_tensor(mine, mine, wide(keep), ALU.mult))
            link(V.tensor_tensor(mine, mine, wide(hide), ALU.add))
            done(V.tensor_reduce(s_max[:, 0:DVE_HEADS], mine, AX_X, ALU.max, negate=True), "s_max")
            pool_s.wait(dve, "conv")
            done(V.tensor_reduce(s_max[:, DVE_HEADS:H], conv[:, DVE_HEADS:H, :], AX_X, ALU.max, negate=True), "s_max_rest")
            for b in range(4):
                pe_s.wait(dve, f"prob_t{b}")
                done(V.tensor_copy(probT[:, 4 * b:4 * b + 4, :], bank[:, b, :].rearrange("p (h t) -> p h t", t=T)),
                     f"probT{b}")
            pe_s.wait(dve, "pv0")
            link(V.reciprocal(s_sum[:, :], s_sum[:, :]))
            heads = lambda a: a.rearrange("p (h d) -> p h d", d=HD)
            spread = lambda a: a.unsqueeze(2).broadcast_to([P, H, HD])
            done(V.tensor_tensor(heads(o0[:, :]), heads(bank[:, 7, 0:D]), spread(s_sum[:, :]), ALU.mult), "o0")
            pe_s.wait(dve, "o0_t")
            done(V.tensor_copy(oT[:, :, :], turned(0)), "o0T")
            pe_s.wait(dve, "proj0")
            done(V.tensor_tensor(x[:, :], x[:, :], bank[:, 1, 0:D], ALU.add), "x1")

            norm_turn(2)
            dve.wait_ge(ld_xw, 32)
            xw, xb = part(x_wts, XW_COLS, "x_w", KD), part(x_wts, XW_COLS, "x_b")
            link(V.tensor_copy(x_high[:, :, :], xw))
            link(V.tensor_tensor(x_low[:, :, :], xw, x_high[:, :, :].bitcast(F32), ALU.subtract))
            link(V.tensor_copy(ident_r[:, :], ident))
            link(V.memset(k_stack0[ONE_ROW:STACK, :, :].bitcast(F32), 1.0))

            def context_high(j):
                dve.wait_ge(c_loaded, 16 * j + 16)
                wait_at(dve, c_proj, 4 * j)
                V.tensor_copy(s_high[:, :, :], s_raw[:, :, :]).then_inc(c_high, 1)

            def keys_low(j, b, u, at=7):
                m, w = divmod(u, 2)
                dve.wait_ge(c_kh, 4 * j + u + 1)
                V.scalar_tensor_tensor(out=k_low[:, b, m, w * SW:(w + 1) * SW], in0=bank[:, at, 0:SW],
                                       scalar=xb[:, m:m + 1], in1=k_high[:, b, m, w * SW:(w + 1) * SW].bitcast(F32),
                                       op0=ALU.add, op1=ALU.subtract).then_inc(c_kl, 1)

            context_high(0)
            pe_s.wait(dve, "qkvh1")
            act_s.wait(dve, "kq1")
            link(V.tensor_tensor(h_beta[:, :], bank[:, 3, 0:D], part(w0, L0_COLS, "beta"), ALU.add))
            done(V.tensor_copy(v_lin[:, :], bank[:, 2, D:2 * D]), "v1")
            pe_s.wait(dve, "kv1")
            link(V.tensor_tensor(kv[:, :, :], turned(5), same_head.unsqueeze(1).broadcast_to([P, KD, P]), ALU.mult))
            link(V.tensor_copy(gT[:, 0, 0:KD], bank[:, 6, 0:KD]))
            done(V.tensor_tensor(k_sum[:, :, :], same_head.unsqueeze(1).broadcast_to([P, KD, P]),
                                 gT[:, 0, 0:KD].unsqueeze(2).broadcast_to([P, KD, P]), ALU.mult), "kv_blocks")
            pe_s.wait(dve, "num_den")
            link(V.reciprocal(den[:, :], bank[:, 1, 0:D]))
            link(V.tensor_tensor(att1[:, :], bank[:, 0, 0:D], den[:, :], ALU.mult))
            layer_norm("_att", att1[:, :])
            link(V.tensor_scalar(att1[:, :], att1[:, :], mv[:, 0:1], rstd[:, :], ALU.subtract, ALU.mult))
            link(V.tensor_tensor(att1[:, :], att1[:, :], part(w0, L0_COLS, "ln_w"), ALU.mult))
            link(V.tensor_tensor(att1[:, :], att1[:, :], part(w0, L0_COLS, "ln_b"), ALU.add))
            done(V.tensor_tensor(att1[:, :], att1[:, :], h_beta[:, :], ALU.mult), "gated1")
            pe_s.wait(dve, "gated1_t")
            done(V.tensor_copy(gT[:, :, :], turned(7)), "gT")
            pe_s.wait(dve, "proj1")
            done(V.scalar_tensor_tensor(out=x[:, :], in0=bank[:, 2, 0:D], scalar=0.0, in1=x[:, :], op0=ALU.max,
                                        op1=ALU.add), "x2")

            norm_turn(3)
            pe_s.wait(dve, "gates")
            link(V.tensor_copy(e_log[:, :], bank[:, 1, 0:E + 1]))
            link(V.max(top8[:, :], e_log[:, 0:E]))
            link(V.max_index(top_at[:, :], top8[:, :], e_log[:, 0:E]))
            link(V.tensor_copy(top_f[:, :], top_at[:, :]))
            done(V.tensor_scalar(g_neg[:, :], top8[:, 0:1], -1.0, None, ALU.mult), "g_neg")
            link(V.tensor_scalar(chosen[:, :], iota, top_f[:, 0:1], None, ALU.is_equal))
            link(V.scalar_tensor_tensor(out=chosen[:, :], in0=iota, scalar=top_f[:, 1:2], in1=chosen[:, :],
                                        op0=ALU.is_equal, op1=ALU.add))
            act_s.wait(dve, "s_gate_e")
            link(V.tensor_tensor(score[:, :], chosen[:, :], e_gate[:, :], ALU.mult))
            link(V.tensor_reduce(g_den[:, :], score[:, :], AX_X, ALU.add))
            link(V.reciprocal(g_den[:, :], g_den[:, :]))
            link(V.tensor_scalar(score[:, :], score[:, :], g_den[:, :], None, ALU.mult))
            link(V.tensor_scalar(s_gate[:, :], s_gate[:, :], 1.0, None, ALU.add))
            link(V.reciprocal(s_gate[:, :], s_gate[:, :]))

            def hidden_units(r):
                act_s.wait(dve, f"silu{r}")
                if r >= 2:
                    pe_s.wait(dve, f"contract{r - 2}")
                done(V.tensor_tensor(hid[:, r % 2], silu[:, r % 2],
                                     bank[:, 3 + 2 * (r % 2), :].rearrange("p (n t) -> p n t", t=T), ALU.mult), f"hid{r}")

            def mix(r):
                pe_s.wait(dve, f"contract{r}")
                last = r == E // ER
                for n in range(1 if last else ER):
                    w = s_gate[:, :] if last else score[:, r * ER + n:r * ER + n + 1]
                    ins = V.scalar_tensor_tensor(out=x[:, :], in0=bank[:, 6 + n // 2, (n % 2) * D:(n % 2 + 1) * D],
                                                 scalar=w, in1=x[:, :], op0=ALU.mult, op1=ALU.add)
                    if last:
                        done(ins, "x3")
                    elif n == ER - 1:
                        done(ins, f"mixed{r}")
                    else:
                        link(ins)

            hidden_units(0)
            for r in range(1, E // ER + 1):
                hidden_units(r)
                for u in range(2 * r - 2, 2 * r):
                    keys_low(u // 4, u // 4, u % 4, at=u % 2)
                if r == 2:
                    context_high(1)
                mix(r - 1)
            mix(E // ER)

            norm_turn(4)
            done(V.memset(k_stack1[ONE_ROW:STACK, :, :].bitcast(F32), 1.0), "stack_ready")
            link(V.memset(neg_max[:, 1, :].bitcast(F32), -MIN_START))
            link(V.memset(alpha_log[:, :], 0.0))
            pe_s.wait(dve, "q4")
            for m in range(KD):
                link(V.tensor_scalar(q_f[:, m], bank[:, 1, m * T:(m + 1) * T], xb[:, m:m + 1], HD ** -0.5, ALU.add,
                                     ALU.mult))
            link(V.tensor_copy(q_h[:, :, :], q_f[:, :, :]))
            done(V.tensor_tensor(q_l[:, :, :], q_f[:, :, :], q_h[:, :, :].bitcast(F32), ALU.subtract), "q4_parts")
            pe_s.wait(dve, "q4_stack")
            pair_rows = part(const, CONST_COLS, "pair_rows")
            stacked = bank[:, 2:4, :].rearrange("p b (g t) -> p (b g) t", t=T)
            for hh in range(2):
                link(V.tensor_scalar(q_base[:, :, hh * T:(hh + 1) * T], stacked, pair_rows[:, hh:hh + 1], None,
                                     ALU.mult))
            link(V.tensor_copy(q_stack[:, 0], q_base[:, :, :].bitcast(F32)))
            done(V.tensor_copy(q_stack[:, 1], q_base[:, :, :].bitcast(F32)), "q_base")
            context_high(2)

            def reduce_unit(j, v):
                h, w = divmod(v, 2)
                dve.wait_ge(c_max, 2 * H * j + v + 1)
                if v == 0:
                    wait_at(dve, c_hm, j)
                V.tensor_reduce(unit_max[:, h, w:w + 1], bank[:, bank_of(MAX_BANKS, v), 0:SW], AX_X, ALU.max,
                                negate=True).then_inc(c_red, 1)

            def new_maxima(j, b, n):
                dve.wait_ge(c_red, 2 * H * j + 2 * H)
                wait_at(dve, c_new, j)
                V.tensor_tensor(head_max[:, :], unit_max[:, :, 0], unit_max[:, :, 1], ALU.min).then_inc(c_hm, 1)
                dve.wait_ge(c_hm, j + 1)
                wait_at(dve, c_al, j)
                V.tensor_tensor(neg_max[:, b, :], neg_max[:, 1 - b, :].bitcast(F32), head_max[:, :],
                                ALU.min).then_inc(c_new, 1)
                dve.wait_ge(c_new, j + 1)
                wait_at(dve, c_alx, j)
                V.tensor_tensor(alpha_log[:, :], neg_max[:, b, :].bitcast(F32), neg_max[:, 1 - b, :].bitcast(F32),
                                ALU.subtract).then_inc(c_al, 1)
                dve.wait_ge(c_nt, j + 1)
                wait_at(dve, c_q[1 - b], 16 * (n + b))
                V.tensor_copy(neg_maxT[:, :], bank[0:H, 7, 0:T]).then_inc(c_ntc, 1)

            flat_acc = acc[:, :, :, :].rearrange("p g h c -> p (g h) c")

            def rescale(j):
                dve.wait_ge(c_alx, j + 1)
                wait_at(dve, c_add, 2 * j)
                V.tensor_tensor(flat_acc, flat_acc, alpha[:, :].unsqueeze(2).broadcast_to([P, H, VW]),
                                ALU.mult).then_inc(c_rs, 1)

            def add_sums(j, half):
                dve.wait_ge(c_ot, 2 * j + half + 1)
                dve.wait_ge(c_rs, j + 1)
                wait_at(dve, c_add, 2 * j + half)
                a = acc[:, 4 * half:4 * half + 4]
                parts = bank[:, 7, :].rearrange("p (g q c) -> p g q c", g=4, q=4)
                V.tensor_tensor(a, a, parts[:, :, 0:4:2, 0:VW], ALU.add).then_inc(c_a1, 1)
                dve.wait_ge(c_a1, 2 * j + half + 1)
                V.tensor_tensor(a, a, parts[:, :, 1:4:2, 0:VW], ALU.add).then_inc(c_add, 1)

            def context_slot(n, b, first=False, more=True, build=True, ahead=True):
                j = 2 * n + b
                for p in range(PAIRS):
                    if build and ahead and p == PART_AT:
                        context_high(j + 3)
                    if more:
                        for v in LATE_UNITS[p]:
                            reduce_unit(j + 1, v)
                    if build:
                        for v in EARLY_UNITS[p]:
                            reduce_unit(j + 2, v)
                    if build and p in KEY_AT:
                        keys_low(j + 2, b, KEY_AT.index(p))
                    if p == SUM1_AT:
                        if not first:
                            add_sums(j - 1, 1)
                        rescale(j)
                    if p == SUM0_AT:
                        add_sums(j, 0)
                    if more and p == MAX_AT:
                        new_maxima(j + 1, 1 - b, n + b)

            for v in range(2 * H):
                reduce_unit(0, v)
            new_maxima(0, 0, 0)
            for v in range(EARLY):
                reduce_unit(1, v)
            context_slot(0, 0, first=True)
            context_slot(0, 1)
            with dve.Fori(1, NJ // 2 - 2) as i:
                for b in range(2):
                    context_slot(i, b)
            context_slot(NJ // 2 - 2, 0)
            context_slot(NJ // 2 - 2, 1, ahead=False)
            context_slot(NJ // 2 - 1, 0, build=False)
            context_slot(NJ // 2 - 1, 1, build=False, more=False)
            add_sums(NJ - 1, 1)
            dve.wait_ge(c_add, 2 * NJ)
            link(V.reciprocal(o_den[:, :], flat_acc[:, :, HD]))
            done(V.tensor_tensor(heads(o1[:, :]), flat_acc[:, :, 0:HD], spread(o_den[:, :]), ALU.mult), "o1")
            pe_s.wait(dve, "o1_t")
            done(V.tensor_copy(o1T[:, :].rearrange("p (b t) -> p b t", b=4), bank[0:HD, 0:4, :]), "o1T")
            pe_s.wait(dve, "proj4")
            done(V.tensor_tensor(x[:, :], x[:, :], bank[:, 1, 0:D], ALU.add), "x5")

            norm_turn(5)
            done(V.tensor_tensor_reduce(sq[:, :], xn[:, :], xn[:, :], 1.0, 0.0, ALU.mult, ALU.add, r_one[:, 0:1]),
                 "ss5")
            pool_s.wait(dve, "rms5")
            dve.wait_ge(ld_l1, 64)
            link(V.tensor_scalar(r_one[:, 2:3], r_one[:, 1:2], D ** -0.5, 1e-8, ALU.mult, ALU.max))
            link(V.reciprocal(r_one[:, 3:4], r_one[:, 2:3]))
            done(V.scalar_tensor_tensor(out=xr[:, :], in0=xn[:, :], scalar=r_one[:, 3:4], in1=part(w1, L1_COLS, "rms"),
                                        op0=ALU.mult, op1=ALU.mult), "xr")
            pe_s.wait(dve, "xr_t")
            done(V.tensor_copy(xrT[:, :, :], turned(1)), "xrT")
            pe_s.wait(dve, "qkv5")
            cos, sin = part(tab, TABLE_COLS, "cos"), part(tab, TABLE_COLS, "sin")
            link(V.tensor_copy(v1[:, :], bank[:, 4, 0:D]))
            link(V.tensor_tensor(rot[:, 1, :], bank[:, 3, :], cos, ALU.mult))
            link(V.tensor_tensor(rot[:, 2, 0::2], bank[:, 3, 1::2], sin[:, 0::2], ALU.mult))
            link(V.tensor_tensor(rot[:, 2, 1::2], bank[:, 3, 0::2], sin[:, 1::2], ALU.mult))
            done(V.tensor_tensor(rot[:, 0, :], rot[:, 1, :], rot[:, 2, :], ALU.add), "rot")
            pe_s.wait(dve, "rot_t")
            link(V.tensor_copy(qkT[:, 0:2, :], bank[:, 6, 0:2 * T].rearrange("p (k t) -> p k t", k=2)))
            head_blocks(k_blocks, bank[:, 6, 2 * T:3 * T], 0)
            head_blocks(k_blocks, bank[:, 6, 3 * T:4 * T], 1, "k_blocks5")
            decay = part(tab, TABLE_COLS, "decay").rearrange("p (h t) -> p h t", t=T)
            for b in range(4):
                pe_s.wait(dve, f"scores5_{b}")
                done(V.tensor_tensor(scoreT[:, 4 * b:4 * b + 4, :],
                                     bank[:, SCORE_BANKS[b], :].rearrange("p (h t) -> p h t", t=T),
                                     decay[:, 4 * b:4 * b + 4, :], ALU.mult), f"scoreT{b}")
            pe_s.wait(dve, "y5")
            yh, y2h = heads(y[:, :]), heads(y2[:, :])
            link(V.tensor_reduce(gn[:, 0, :], heads(bank[:, 6, 0:D]), AX_X, ALU.add))
            link(V.tensor_scalar(gn[:, 0, :], gn[:, 0, :], 1.0 / HD, None, ALU.mult))
            link(V.tensor_tensor(yh, heads(bank[:, 6, 0:D]), spread(gn[:, 0, :]), ALU.subtract))
            link(V.tensor_tensor(y2h, yh, yh, ALU.mult))
            link(V.tensor_reduce(gn[:, 1, :], y2h, AX_X, ALU.add))
            done(V.tensor_scalar(gn[:, 1, :], gn[:, 1, :], 1.0 / HD, LN_EPS, ALU.mult, ALU.add), "gn_var")
            pool_s.wait(dve, "gn_rstd")
            link(V.tensor_tensor(yh, yh, spread(gn[:, 2, :]), ALU.mult))
            link(V.tensor_tensor(y[:, :], y[:, :], part(w1, L1_COLS, "gn_w"), ALU.mult))
            link(V.tensor_tensor(y[:, :], y[:, :], part(w1, L1_COLS, "gn_b"), ALU.add))
            act_s.wait(dve, "gate1")
            done(V.tensor_tensor(y[:, :], y[:, :], gate1[:, :], ALU.mult), "y5n")
            pe_s.wait(dve, "y5_t")
            done(V.tensor_copy(yT[:, :, :], turned(0)), "yT")
            pe_s.wait(dve, "proj5")
            link(V.tensor_tensor(x[:, :], x[:, :], xn[:, :], ALU.add))
            done(V.tensor_tensor(x[:, :], x[:, :], bank[:, 1, 0:D], ALU.add), "x5b")

            norm_turn(6)
            pe_s.wait(dve, "p6")
            done(V.tensor_copy(pT[:, :], bank[0:64, 1, 0:T]), "pT")
            pe_s.wait(dve, "q6")
            done(V.tensor_copy(qT2[:, :], bank[0:64, 4, 0:T]), "qT2")
            pe_s.wait(dve, "out6")
            done(V.tensor_tensor(x[:, :], x[:, :], bank[:, 5, 0:D], ALU.add), "x6")


def kernel(**inputs):
    import concourse.bacc as bacc
    from concourse.bass_utils import run_bass_kernel_spmd

    a = {k: np.ascontiguousarray(v) for k, v in inputs.items()}

    def tiles(w):
        k, n = w.shape
        return w.reshape(k // P, P, n).transpose(1, 0, 2).reshape(P, -1)

    def column(v):
        return v.reshape(-1, P).T

    def row(v):
        return np.broadcast_to(v.reshape(1, -1), (P, v.size))

    by_head = np.arange(D).reshape(HD, H).T.reshape(-1)
    X, A, F = "L0_xattn_", "L0_attn_", "L0_ffn_"
    hist = np.concatenate([tiles(a[X + "hist_W"]), tiles(a[X + "ctx_W1"]), a[X + "ctx_W2"], column(a[X + "hist_b"]),
                           column(a[X + "hist_ln_g"]), column(a[X + "hist_ln_b"]), column(a[X + "ctx_b1"]),
                           row(a[X + "ctx_b2"])], 1)
    kvh = np.concatenate([a[A + n][:, by_head] for n in ("Wk", "Wv", "Wh")], 1)
    l0 = np.concatenate([
        tiles(a[X + "Wq"]), tiles(a[X + "Wk"]), tiles(a[X + "Wv"]), tiles(a[X + "proj_W"]), tiles(a[X + "kg_W1"]),
        tiles(a[X + "kg_W2"]), tiles(kvh), tiles(a[A + "Wq"][:, by_head]), tiles(a[A + "Wo"][by_head, :]),
        tiles(np.concatenate([a[F + "Wg"].T, a[F + "Wsg"].T], 1)), column(a[A + "bq"][by_head]),
        row(a[X + "kg_ln_g"]), row(a[X + "kg_ln_b"]), row(a[A + "beta"][by_head]), row(a[A + "ln_w"][by_head]),
        row(a[A + "ln_b"][by_head])], 1)
    rows0 = np.concatenate([a[X + "kg_b1"], a[X + "kg_b2"], a[X + "proj_b"]]
                           + [a[A + n][by_head] for n in ("bk", "bv", "bh")] + [a[A + "bo"]])[None]
    ffn = np.concatenate([
        tiles(a[F + "We_gate"].reshape(E * P, D).T), tiles(a[F + "We_up"].reshape(E * P, D).T),
        a[F + "We_down"].transpose(2, 0, 1).reshape(P, E * D), tiles(a[F + "Ws_gate"].T), tiles(a[F + "Ws_up"].T),
        tiles(a[F + "Ws_down"].T)], 1)
    spare = np.zeros((P, L0_PIECES * L0_PIECE - N_L0 - N_FFN), np.float32)
    l0 = np.concatenate([l0, ffn, spare], 1)
    C, R, L = "L1_xattn_", "L1_attn_", "L1_ffn_"
    order = head_columns()
    qkvff = a[R + "w_qkvff"].T
    xw = np.concatenate([tiles(a[C + "Wq"].T[:, order]), column(a[C + "bq"][order])], 1)
    l1 = np.concatenate([
        tiles(qkvff[:, :3 * D]), tiles(qkvff[:, 3 * D:]), tiles(a[R + "w_gated"].T), tiles(a[R + "w_proj"].T),
        tiles(a[R + "w_ff"].T), row(a[R + "rms_w"]), row(a[R + "gn_w"]), row(a[R + "gn_b"]), tiles(a[L + "U1"]),
        column(a[L + "b1"]), tiles(a[L + "U2"])], 1)
    rows1 = np.concatenate([a[R + "b_gated"], a[R + "b_proj"], a[L + "b2"]])[None]
    arrays = {
        "ctx_t": a["ctx_1024"][0].T, "x": a["x"][0], "mask": a["mask_SxS_bc0"].view(np.uint32), "const": constants(),
        "hist": hist, "l0": l0, "rows0": rows0, "xw": xw, "x_bo": a[C + "bo"][None], "x_o": a[C + "Wo"].T, "l1": l1, "rows1": rows1,
        "v": np.concatenate([a[L + "V1"], a[L + "V2"]], 1), "tables": tables(),
    }
    arrays = {k: np.ascontiguousarray(v) for k, v in arrays.items()}
    nc = bacc.Bacc("TRN2", target_bir_lowering=False, num_devices=1)
    args = [nc.dram_tensor("in_" + k, v.shape, mybir.dt.from_np(v.dtype), kind="ExternalInput").ap() for k, v in arrays.items()]
    out = nc.dram_tensor("out_x", (T, D), F32, kind="ExternalOutput").ap()
    build_kernel(nc, *args, out)
    result = run_bass_kernel_spmd(nc, [{"in_" + k: v for k, v in arrays.items()}], core_ids=[0])
    return result.results[0]["out_x"].reshape(1, T, D)
```
